# Optimizing a Trainium2 kernel written in Bass

```python
import numpy as np
import jax
import jax.numpy as jnp

def _softmax(x, axis=-1):
    return jax.nn.softmax(x, axis=axis)

def _gelu(x):
    return jax.nn.gelu(x, approximate=True)

def _silu(x):
    return jax.nn.silu(x)

def _sigmoid(x):
    return jax.nn.sigmoid(x)

def _layernorm(x, axis=-1, eps=1e-05):
    m = jnp.mean(x, axis=axis, keepdims=True)
    v = jnp.var(x, axis=axis, keepdims=True)
    return (x - m) / jnp.sqrt(v + eps)

def _scatter_add(tgt, idx, src, axis=0):
    return tgt.at[idx].add(src)

def _segment_sum(src, seg, n):
    return jax.ops.segment_sum(src, seg, n)
kernel_name = 'mk_lm_tower_d1_tok_ids1024_r4_34e422'

def setup_inputs(seed: int=0):
    np.random.seed(seed)
    _w = jnp.asarray

    def _rec_inputs():
        import jax
        import jax.numpy as jnp
        _rk = jax.random.key(seed)
        x = jax.random.randint(jax.random.fold_in(_rk, 1), (16, 128), 0, 200, jnp.int32)
        return x
    x = _rec_inputs()

    def _L0_tok_setup():
        import jax, jax.numpy as jnp
        import numpy as np
        NUM_LEVELS = 32
        SCALE = 0.15
        OPEN_TOKENS = jnp.array([40, 91, 123], dtype=jnp.int32)
        CLOSE_TOKENS = jnp.array([41, 93, 125], dtype=jnp.int32)

        def _compute_levels(token_ids, num_levels):
            is_open = (token_ids[..., None] == OPEN_TOKENS).any(-1)
            is_close = (token_ids[..., None] == CLOSE_TOKENS).any(-1)
            delta = is_open.astype(jnp.int32) - is_close.astype(jnp.int32)

            def step(lvl, d):
                lvl = jnp.clip(lvl + d, 0, num_levels - 1)
                return (lvl, lvl)
            init = jnp.zeros(token_ids.shape[0], dtype=jnp.int32)
            _, levels = jax.lax.scan(step, init, delta.T)
            return levels.T
        key = jax.random.key(seed)
        k1, k2 = jax.random.split(key)
        token_ids = jax.random.randint(k1, (8, 2048), 0, 200, dtype=jnp.int32)
        level_emb = jax.random.normal(k2, (NUM_LEVELS, 256), dtype=jnp.float32)
        return {'token_ids': token_ids, 'level_emb': level_emb}
    _L0_tok_all = _L0_tok_setup()
    _L0_tok_in = {k: v for k, v in _L0_tok_all.items() if k in ('level_emb',)}
    del _L0_tok_all

    def _L0_attn_setup():
        import math
        import jax, jax.numpy as jnp
        import numpy as np
        D_MODEL = 256
        NUM_Q_HEADS = 16
        NUM_KV_HEADS = 4
        HEAD_DIM = D_MODEL // NUM_Q_HEADS
        GROUP_SIZE = NUM_Q_HEADS // NUM_KV_HEADS
        KV_DIM = NUM_KV_HEADS * HEAD_DIM
        key = jax.random.key(seed)
        ks = jax.random.split(key, 9)
        s = 0.02
        x = jax.random.normal(ks[0], (1, 1024, D_MODEL), dtype=jnp.float32)
        Wq = jax.random.normal(ks[1], (D_MODEL, D_MODEL), dtype=jnp.float32) * s
        bq = jax.random.normal(ks[2], (D_MODEL,), dtype=jnp.float32) * s
        Wk = jax.random.normal(ks[3], (D_MODEL, KV_DIM), dtype=jnp.float32) * s
        bk = jax.random.normal(ks[4], (KV_DIM,), dtype=jnp.float32) * s
        Wv = jax.random.normal(ks[5], (D_MODEL, KV_DIM), dtype=jnp.float32) * s
        bv = jax.random.normal(ks[6], (KV_DIM,), dtype=jnp.float32) * s
        Wo = jax.random.normal(ks[7], (D_MODEL, D_MODEL), dtype=jnp.float32) * s
        bo = jax.random.normal(ks[8], (D_MODEL,), dtype=jnp.float32) * s
        return {'x': x, 'Wq': Wq, 'bq': bq, 'Wk': Wk, 'bk': bk, 'Wv': Wv, 'bv': bv, 'Wo': Wo, 'bo': bo}
    _L0_attn_all = _L0_attn_setup()
    _L0_attn_in = {k: v for k, v in _L0_attn_all.items() if k in ('Wq', 'bq', 'Wk', 'bk', 'Wv', 'bv', 'Wo', 'bo')}
    del _L0_attn_all

    def _L0_ffn_setup():
        import jax, jax.numpy as jnp
        import numpy as np
        EPS = 1e-05

        def _quantize(W):
            gamma = jnp.mean(jnp.abs(W))
            return jnp.clip(jnp.round(W / (gamma + EPS)), -1.0, 1.0)
        key = jax.random.key(seed)
        k_x, k_w1, k_b1, k_w2, k_b2 = jax.random.split(key, 5)
        n_embd = 256
        d_ff = 4 * n_embd
        B, S = (4, 1024)
        bound1 = 1.0 / np.sqrt(n_embd)
        bound2 = 1.0 / np.sqrt(d_ff)
        x = jax.random.normal(k_x, (B, S, n_embd), dtype=jnp.float32)
        W1 = jax.random.uniform(k_w1, (d_ff, n_embd), jnp.float32, -bound1, bound1)
        b1 = jax.random.uniform(k_b1, (d_ff,), jnp.float32, -bound1, bound1)
        W2 = jax.random.uniform(k_w2, (n_embd, d_ff), jnp.float32, -bound2, bound2)
        b2 = jax.random.uniform(k_b2, (n_embd,), jnp.float32, -bound2, bound2)
        return {'x': x, 'W1': W1, 'b1': b1, 'W2': W2, 'b2': b2}
    _L0_ffn_all = _L0_ffn_setup()
    _L0_ffn_in = {k: v for k, v in _L0_ffn_all.items() if k in ('W1', 'b1', 'W2', 'b2')}
    del _L0_ffn_all
    return {'x': x, 'L0_tok_level_emb': _L0_tok_in['level_emb'], 'L0_attn_Wq': _L0_attn_in['Wq'], 'L0_attn_bq': _L0_attn_in['bq'], 'L0_attn_Wk': _L0_attn_in['Wk'], 'L0_attn_bk': _L0_attn_in['bk'], 'L0_attn_Wv': _L0_attn_in['Wv'], 'L0_attn_bv': _L0_attn_in['bv'], 'L0_attn_Wo': _L0_attn_in['Wo'], 'L0_attn_bo': _L0_attn_in['bo'], 'L0_ffn_W1': _L0_ffn_in['W1'], 'L0_ffn_b1': _L0_ffn_in['b1'], 'L0_ffn_W2': _L0_ffn_in['W2'], 'L0_ffn_b2': _L0_ffn_in['b2']}

def reference(x, L0_tok_level_emb, L0_attn_Wq, L0_attn_bq, L0_attn_Wk, L0_attn_bk, L0_attn_Wv, L0_attn_bv, L0_attn_Wo, L0_attn_bo, L0_ffn_W1, L0_ffn_b1, L0_ffn_W2, L0_ffn_b2):
    import jax
    import jax.numpy as jnp

    def _L0_tok_ref(token_ids, level_emb):
        import jax, jax.numpy as jnp
        import numpy as np
        NUM_LEVELS = 32
        SCALE = 0.15
        OPEN_TOKENS = jnp.array([40, 91, 123], dtype=jnp.int32)
        CLOSE_TOKENS = jnp.array([41, 93, 125], dtype=jnp.int32)

        def _compute_levels(token_ids, num_levels):
            is_open = (token_ids[..., None] == OPEN_TOKENS).any(-1)
            is_close = (token_ids[..., None] == CLOSE_TOKENS).any(-1)
            delta = is_open.astype(jnp.int32) - is_close.astype(jnp.int32)

            def step(lvl, d):
                lvl = jnp.clip(lvl + d, 0, num_levels - 1)
                return (lvl, lvl)
            init = jnp.zeros(token_ids.shape[0], dtype=jnp.int32)
            _, levels = jax.lax.scan(step, init, delta.T)
            return levels.T
        levels = _compute_levels(token_ids, NUM_LEVELS)
        hierarchy_pos = level_emb[levels]
        return hierarchy_pos * SCALE

    def _L0_attn_ref(x, Wq, bq, Wk, bk, Wv, bv, Wo, bo):
        import math
        import jax, jax.numpy as jnp
        import numpy as np
        D_MODEL = 256
        NUM_Q_HEADS = 16
        NUM_KV_HEADS = 4
        HEAD_DIM = D_MODEL // NUM_Q_HEADS
        GROUP_SIZE = NUM_Q_HEADS // NUM_KV_HEADS
        KV_DIM = NUM_KV_HEADS * HEAD_DIM
        b, s, _ = x.shape
        q = (x @ Wq + bq).reshape(b, s, NUM_Q_HEADS, HEAD_DIM).transpose(0, 2, 1, 3)
        k = (x @ Wk + bk).reshape(b, s, NUM_KV_HEADS, HEAD_DIM).transpose(0, 2, 1, 3)
        v = (x @ Wv + bv).reshape(b, s, NUM_KV_HEADS, HEAD_DIM).transpose(0, 2, 1, 3)
        k = jnp.repeat(k, GROUP_SIZE, axis=1)
        v = jnp.repeat(v, GROUP_SIZE, axis=1)
        scores = jnp.einsum('bhqd,bhkd->bhqk', q, k) / math.sqrt(HEAD_DIM)
        attn = jax.nn.softmax(scores, axis=-1)
        context = jnp.einsum('bhqk,bhkd->bhqd', attn, v)
        context = context.transpose(0, 2, 1, 3).reshape(b, s, D_MODEL)
        return context @ Wo + bo

    def _L0_ffn_ref(x, W1, b1, W2, b2):
        import jax, jax.numpy as jnp
        import numpy as np
        EPS = 1e-05

        def _quantize(W):
            gamma = jnp.mean(jnp.abs(W))
            return jnp.clip(jnp.round(W / (gamma + EPS)), -1.0, 1.0)
        Wq1 = _quantize(W1)
        Wq2 = _quantize(W2)
        h = jax.nn.relu(jnp.einsum('bsd,fd->bsf', x, Wq1) + b1)
        out = jnp.einsum('bsf,df->bsd', h, Wq2) + b2
        return out
    h = _L0_tok_ref(x, L0_tok_level_emb)
    h = h + _L0_attn_ref(_layernorm(h, axis=-1), L0_attn_Wq, L0_attn_bq, L0_attn_Wk, L0_attn_bk, L0_attn_Wv, L0_attn_bv, L0_attn_Wo, L0_attn_bo)
    h = h + _L0_ffn_ref(_layernorm(h, axis=-1), L0_ffn_W1, L0_ffn_b1, L0_ffn_W2, L0_ffn_b2)
    return h

_drawn_inputs = setup_inputs


def setup_inputs(seed=0):
    import zlib

    import numpy as np

    out = dict(_drawn_inputs(seed))
    spreads = {}
    factors = {'L0_attn_Wq': 2.892,
     'L0_attn_bq': 8.0,
     'L0_attn_Wk': 2.967,
     'L0_attn_bk': 64.0,
     'L0_ffn_b1': 24.949,
     'L0_ffn_b2': 64.0}
    for name, (base, spread) in spreads.items():
        noise = np.random.default_rng([zlib.crc32(name.encode()), seed]).standard_normal(out[name].shape)
        drawn = base * np.exp(spread * noise) if base else spread * noise
        out[name] = jnp.asarray(drawn.astype(out[name].dtype))
    for name, factor in factors.items():
        out[name] = (out[name] * factor).astype(out[name].dtype)
    return out
```

```python
from contextlib import ExitStack

import concourse.bass as bass
from concourse import mybir

F32 = mybir.dt.float32
F32R = mybir.dt.float32r
BF16 = mybir.dt.bfloat16
I32 = mybir.dt.int32
ALU = mybir.AluOpType
ACT = mybir.ActivationFunctionType
AX_X = mybir.AxisListType.X

P = 128
OPEN_TOKENS = (40, 91, 123)
CLOSE_TOKENS = (41, 93, 125)
EMB_SCALE = 0.15
EPS = 1e-5
ABSENT = -1e30


def level_tower(nc, x, emb, Wq, bq, Wk, bk, Wv, bv, Wo, bo, W1, b1, W2, b2, out):
    B, S = x.shape
    L, D = emb.shape
    KVD = Wk.shape[1]
    HD = 16
    KV = KVD // HD
    G = D // HD // KV
    F = W1.shape[0]
    KC = D // P
    FC = F // P
    BG = P // L
    NG = B // BG
    HALF = NG // 2
    H2 = G // 2
    GB = BG * KV
    RH = HALF * P
    VW = KVD + KV
    SCALE = float(HD) ** -0.5
    assert S == P and L == 32 and D == 2 * P and G == 4 and KV == 4 and NG == 4 and F % P == 0

    ctx = ExitStack()
    with ctx:
        def sb(name, shape, dt=F32):
            return ctx.enter_context(nc.sbuf_tensor(name, shape, dt))

        def sem(name):
            return ctx.enter_context(nc.semaphore(name))

        pswt = [ctx.enter_context(nc.psum_tensor(f"pswt{i}", [P, 512], F32)) for i in range(2)]
        psmisc = [ctx.enter_context(nc.psum_tensor(f"psmisc{i}", [P, 512], F32)) for i in range(2)]
        psg = [ctx.enter_context(nc.psum_tensor(f"psg{i}", [P, 512], F32)) for i in range(NG)]

        tok = sb("tok", [B, S], I32)
        emb4 = sb("emb4", [P, D])
        wq = sb("wq", [P, KC, D])
        wqh = sb("wqh", [P, KC, G, 2, KVD])
        wk = sb("wk", [P, KC, 2, KVD])
        wv = sb("wv", [P, KC, KVD])
        brow = sb("brow", [1, D])
        bqr = sb("bqr", [1, G, 2, KVD])
        bkr = sb("bkr", [1, 2, KVD])
        bvr = sb("bvr", [1, KVD])
        wo = sb("wo", [P, H2, D])
        bo_bc = sb("bo_bc", [P, D])
        b2_bc = sb("b2_bc", [P, D])
        b1c = sb("b1c", [P, FC])
        w1 = sb("w1", [P, FC, D])
        w2 = sb("w2", [P, KC, F])
        identf = sb("identf", [P, P])
        identb = sb("identb", [P, P], BF16)
        nidentb = sb("nidentb", [P, P], BF16)
        ones = sb("ones", [P, P])
        sel4 = sb("sel4", [64, 512], F32R)
        selb = sb("selb", [B, 512], BF16)
        bm = sb("bm", [P, BG])
        km = sb("km", [P, KV])
        pidx = sb("pidx", [P, 1], I32)
        pint = sb("pint", [P, 3], I32)
        pnum = sb("pnum", [P, 3])
        ridx = sb("ridx", [P, P], I32)
        rmod = sb("rmod", [P, P], I32)
        jdx = sb("jdx", [P, 512], I32)
        rep = sb("rep", [P, P], BF16)
        mhalf = sb("mhalf", [P, 1])
        cmp = sb("cmp", [B, 5, S])
        sc0 = sb("sc0", [B, 2 * S])
        sc1 = sb("sc1", [B, 2 * S])
        lev = sb("lev", [B, 2 * S], BF16)
        oh = sb("oh", [P, NG, S], F32R)
        cnt = sb("cnt", [P, NG])
        neg = sb("neg", [P, NG], BF16)
        cb = sb("cb", [P, NG, BG], BF16)
        cpos = sb("cpos", [P, B])
        cabs = sb("cabs", [P, B])
        lnc0 = sb("lnc0", [P, B])
        lnc = sb("lnc", [P, B])
        h0 = sb("h0", [P, D])
        st1 = sb("st1", [P, 6])
        mv1 = sb("mv1", [P, 2])
        ve1 = sb("ve1", [P, 1])
        rs1 = sb("rs1", [P, 1])
        xn1 = sb("xn1", [P, D])
        xT1 = sb("xT1", [P, KC, P])
        qs = sb("qs", [P, P], F32R)
        ktm = sb("ktm", [P, P])
        khi = sb("khi", [P, P], F32R)
        klo = sb("klo", [P, P], F32R)
        vo = sb("vo", [P, VW])
        eb = sb("eb", [P, D])
        mx = sb("mx", [P, NG, GB])
        mxr = sb("mxr", [P, NG, 64], F32R)
        ms = sb("ms", [64, NG, P], F32R)
        et = sb("et", [P, NG, BG, P])
        rec = sb("rec", [P, NG, GB])
        cn = sb("cn", [P, NG, BG * KVD])
        cT = sb("cT", [P, NG, H2, BG, L])
        hq = sb("hq", [P, NG, D])
        hb = sb("hb", [P, NG, D])
        st2 = sb("st2", [P, NG, 6])
        mv2 = sb("mv2", [P, NG, 2])
        ve2 = sb("ve2", [P, NG])
        rs2 = sb("rs2", [P, NG])
        xn2 = sb("xn2", [P, NG, D])
        xhi = sb("xhi", [P, KC, NG, P], F32R)
        xlo = sb("xlo", [P, KC, NG, P], F32R)
        asum = sb("asum", [P, 4])
        ascr = sb("ascr", [P, 1024])
        thr = sb("thr", [P, 4])
        tpos = sb("tpos", [P, 2, 2048], BF16)
        tneg = sb("tneg", [P, 2, 2048], BF16)
        w1T = sb("w1T", [P, FC, KC, P], F32R)
        w2T = sb("w2T", [P, FC, D], F32R)
        NHB = 3
        hr = sb("hr", [P, NHB, RH])
        hh = sb("hh", [P, NHB, RH], F32R)
        hl = sb("hl", [P, NHB, RH], F32R)
        fin = sb("fin", [P, NG, D])
        fhi = sb("fhi", [P, NG, D], F32R)
        flo = sb("flo", [P, NG, D], F32R)
        osb = sb("osb", [P, NG, BG, D])

        d_tok, d_emb, d_wq, d_wk, d_wv, d_bq, d_bk, d_bv = (sem("d_" + n) for n in "tok emb wq wk wv bq bk bv".split())
        d_bo, d_b1, d_b2 = (sem("d_" + n) for n in "bo b1 b2".split())
        d_w1 = [sem(f"d_w1_{i}") for i in range(2)]
        d_w2 = [sem(f"d_w2_{i}") for i in range(2)]
        d_wo = [sem(f"d_wo_{i}") for i in range(4)]
        d_out = sem("d_out")

        c_ones = sem("c_ones")
        c_iota = sem("c_iota")
        c_misc = sem("c_misc")
        c_pnum = sem("c_pnum")
        c_ident = sem("c_ident")
        c_sel = sem("c_sel")
        c_bm = sem("c_bm")
        c_mod = sem("c_mod")
        c_rep = sem("c_rep")
        c_scan = sem("c_scan")
        v_delta = sem("v_delta")
        v_lev = sem("v_lev")
        p_lev = sem("p_lev")
        v_oh = sem("v_oh")
        v_cnt = sem("v_cnt")
        v_neg = sem("v_neg")
        v_cb = sem("v_cb")
        p_cnt = sem("p_cnt")
        v_cpos = sem("v_cpos")
        a_ln = sem("a_ln")
        v_lnc = sem("v_lnc")
        v_h0 = sem("v_h0")
        v_st1 = sem("v_st1")
        v_mv1 = sem("v_mv1")
        v_ve1 = sem("v_ve1")
        g_rs1 = sem("g_rs1")
        v_xn1 = sem("v_xn1")
        p_xT1 = sem("p_xT1")
        a_xT1 = sem("a_xT1")
        p_k = sem("p_k")
        p_q = sem("p_q")
        p_v = sem("p_v")
        v_ktm = sem("v_ktm")
        v_khi = sem("v_khi")
        v_klo = sem("v_klo")
        v_qhi = sem("v_qhi")
        v_qs = sem("v_qs")
        v_vo = sem("v_vo")
        g_eb = sem("g_eb")
        g_bqr = sem("g_bqr")
        g_wqh = sem("g_wqh")
        a_wqh = sem("a_wqh")
        p_s = sem("p_s")
        v_mx = sem("v_mx")
        p_mt = sem("p_mt")
        a_ms = sem("a_ms")
        v_mhi = sem("v_mhi")
        v_mlo = sem("v_mlo")
        p_et = sem("p_et")
        a_exp = sem("a_exp")
        p_ctx = sem("p_ctx")
        v_rec = sem("v_rec")
        v_cn = sem("v_cn")
        p_cT = sem("p_cT")
        a_cT = sem("a_cT")
        p_wo = sem("p_wo")
        v_hq = sem("v_hq")
        g_hb = sem("g_hb")
        v_st2 = sem("v_st2")
        v_mv2 = sem("v_mv2")
        v_ve2 = sem("v_ve2")
        g_rs2 = sem("g_rs2")
        v_xn2 = sem("v_xn2")
        p_xT2 = sem("p_xT2")
        a_xhi = sem("a_xhi")
        v_xlo = sem("v_xlo")
        v_abs = sem("v_abs")
        a_abs = sem("a_abs")
        p_gam = [sem(f"p_gam{i}") for i in range(2)]
        v_thr = sem("v_thr")
        v_tern = sem("v_tern")
        p_wt = sem("p_wt")
        a_wt = sem("a_wt")
        p_f1 = sem("p_f1")
        a_hr = sem("a_hr")
        v_hh = sem("v_hh")
        v_hl = sem("v_hl")
        p_f2 = sem("p_f2")
        p_acc = sem("p_acc")
        v_fin = sem("v_fin")
        v_fhi = sem("v_fhi")
        v_flo = sem("v_flo")
        p_out = sem("p_out")
        a_out = sem("a_out")
        v_out = sem("v_out")

        block = ctx.enter_context(nc.Block())

        w1_rows = W1.rearrange("(p j) d -> p j d", j=FC)
        w2_rows = W2.rearrange("(c p) f -> p c f", p=P)
        wo_rows = Wo.rearrange("(k a e d) n -> a e k d n", k=KV, a=2, e=H2)

        @block.sync
        def _(sp):
            sp.dma_start(tok[:], x).then_inc(d_tok, 16)
            sp.dma_start(emb4[:], emb.unsqueeze(0).to_broadcast([BG, L, D])).then_inc(d_emb, 16)
            for r in range(2):
                sp.dma_start(wk[:, :, r, :], Wk.rearrange("(c p) n -> p c n", p=P)).then_inc(d_wk, 16)
            sp.dma_start(wq[:], Wq.rearrange("(c p) n -> p c n", p=P)).then_inc(d_wq, 16)
            sp.dma_start(wv[:], Wv.rearrange("(c p) n -> p c n", p=P)).then_inc(d_wv, 16)
            for i in range(2):
                c = slice(i * FC // 2, (i + 1) * FC // 2)
                sp.dma_start(w1[:, c, :], w1_rows[:, c, :]).then_inc(d_w1[i], 16)
            for i in range(2):
                sp.dma_start(w2[:, i, :], w2_rows[:, i, :]).then_inc(d_w2[i], 16)
            out_t = out.rearrange("b s d -> s b d")
            for g in range(NG):
                for e in range(2):
                    if e == 0:
                        sp.wait_ge(a_out, g + 1)
                    else:
                        sp.wait_ge(v_out, g + 1)
                    b0 = g * BG + 2 * e
                    sp.dma_start(out_t[:, b0:b0 + 2, :], osb[:, g, 2 * e:2 * e + 2, :]).then_inc(d_out, 16)
            sp.wait_ge(d_out, 16 * 2 * NG)

        @block.gpsimd
        def _(pool):
            nc.gpsimd.memset(sc0[:], 0.0).then_inc(c_scan, 1)
            nc.gpsimd.memset(sc1[:], 0.0).then_inc(c_scan, 1)
            pool.wait_ge(c_scan, 2)
            nc.gpsimd.memset(sc1[:].rearrange("b (s e) -> b s e", e=2)[:, :, 0:1], float(1 - L)).then_inc(c_scan, 1)
            nc.gpsimd.iota(pidx[:], pattern=[[0, 1]], base=0, channel_multiplier=1).then_inc(c_iota, 1)
            nc.gpsimd.iota(ridx[:], pattern=[[-1, P]], base=P, channel_multiplier=1).then_inc(c_iota, 1)
            nc.gpsimd.iota(jdx[:], pattern=[[1, GB], [0, L]], base=0, channel_multiplier=0).then_inc(c_iota, 1)
            nc.gpsimd.memset(ones[:], 1.0).then_inc(c_ones, 1)
            nc.gpsimd.memset(mhalf[:], -0.5).then_inc(c_misc, 1)
            nc.gpsimd.memset(mxr[:].bitcast(F32), 0.0).then_inc(c_misc, 1)
            pool.wait_ge(d_bq, 16)
            for r in range(2):
                nc.gpsimd.tensor_copy(bqr[0:1, :, r, :].rearrange("p h (k d) -> p h k d", k=KV),
                                      brow[:].rearrange("p (k h d) -> p h k d", k=KV, h=G)).then_inc(g_bqr, 1)
            pool.wait_ge(d_wq, 16)
            for r in range(2):
                nc.gpsimd.tensor_copy(wqh[:, 0, :, r, :].rearrange("p h (k d) -> p h k d", k=KV),
                    wq[:, 0, :].rearrange("p (k h d) -> p h k d", k=KV, h=G)).then_inc(g_wqh, 1)
            pool.wait_ge(v_ve1, 1)
            pool.wait_ge(c_misc, 2)
            nc.gpsimd.tensor_tensor(rs1[:], ve1[:], mhalf[:], ALU.pow).then_inc(g_rs1, 1)
            pool.wait_ge(v_h0, 1)
            pool.wait_ge(d_bo, 16)
            nc.gpsimd.tensor_tensor(eb[:], h0[:], bo_bc[:], ALU.add).then_inc(g_eb, 1)
            pool.wait_ge(d_b2, 16)
            for g in range(NG):
                pool.wait_ge(v_ve2, g + 1)
                nc.gpsimd.tensor_tensor(rs2[:, g:g + 1], ve2[:, g:g + 1], mhalf[:], ALU.pow).then_inc(g_rs2, 1)
                nc.gpsimd.tensor_tensor(hb[:, g, :], hq[:, g, :], b2_bc[:], ALU.add).then_inc(g_hb, 1)

        @block.scalar
        def _(act):
            act.dma_start(bkr[:], bk.unsqueeze(0).unsqueeze(0).to_broadcast([1, 2, KVD])).then_inc(d_bk, 16)
            act.dma_start(brow[:], bq.unsqueeze(0)).then_inc(d_bq, 16)
            act.dma_start(bvr[:], bv.unsqueeze(0)).then_inc(d_bv, 16)
            act.dma_start(bo_bc[:], bo.unsqueeze(0).to_broadcast([P, D])).then_inc(d_bo, 16)
            for a in range(2):
                for e in range(H2):
                    act.dma_start(wo[64 * a:64 * a + 64, e, :], wo_rows[a, e]).then_inc(d_wo[2 * a + e], 16)
            act.dma_start(b1c[:], b1.rearrange("(p j) -> p j", j=FC)).then_inc(d_b1, 16)
            act.dma_start(b2_bc[:], b2.unsqueeze(0).to_broadcast([P, D])).then_inc(d_b2, 16)

            act.wait_ge(d_wq, 16)
            for r in range(2):
                nc.scalar.activation(wqh[:, 1, :, r, :].rearrange("p h (k d) -> p h k d", k=KV),
                    wq[:, 1, :].rearrange("p (k h d) -> p h k d", k=KV, h=G), ACT.Copy).then_inc(a_wqh, 1)
            act.wait_ge(p_xT1, 1)
            nc.scalar.activation(xT1[:], psmisc[0][:, 0:KC * P].rearrange("p (k n) -> p k n", k=KC), ACT.Copy).then_inc(a_xT1, 1)

            def abs_sum(w, i):
                src = w1[:, FC // 2:, :].rearrange("p j d -> p (j d)") if w == 0 else w2[:, 1, :]
                act.wait_ge((d_w1, d_w2)[w][1], 16)
                if w:
                    act.wait_ge(a_abs, 1)
                nc.scalar.activation(ascr[:], src, ACT.Abs, accum_out=asum[:, 2 * w + 1:2 * w + 2]).then_inc(a_abs, 1)

            def weights_out(u):
                act.wait_ge(p_wt, u + 1)
                src = pswt[u % 2][:, :]
                j = 2 * (u % 4)
                if u < 4:
                    nc.scalar.activation(w1T[:, j:j + 2, :, :].rearrange("p j k f -> p (j k f)"), src, ACT.Copy).then_inc(a_wt, 1)
                else:
                    nc.scalar.activation(w2T[:, j:j + 2, :].rearrange("p j d -> p (j d)"), src, ACT.Copy).then_inc(a_wt, 1)

            def max_out(g):
                act.wait_ge(p_mt, g + 1)
                nc.scalar.activation(ms[:, g, :], psmisc[g % 2][0:64, 0:P], ACT.Copy).then_inc(a_ms, 1)

            def exps(g):
                act.wait_ge(p_et, g + 1)
                act.wait_ge(v_lnc, 1)
                for b in range(BG):
                    n = g * BG + b
                    nc.scalar.activation(et[:, g, b, :], psg[g][:, b * P:(b + 1) * P], ACT.Exp,
                                         bias=lnc[:, n:n + 1]).then_inc(a_exp, 1)

            def ctx_out(g):
                act.wait_ge(p_cT, g + 1)
                src = psg[g][0:64, :].rearrange("p (b a e l) -> p a b e l", b=BG, a=2, e=H2)
                for a in range(2):
                    dst = cT[64 * a:64 * a + 64, g].rearrange("p e b l -> p b e l")
                    nc.scalar.activation(dst, src[:, a], ACT.Copy).then_inc(a_cT, 1)

            def x_hi(g):
                act.wait_ge(p_xT2, g + 1)
                nc.scalar.activation(xhi[:, :, g, :], psg[g][:, 0:KC * P].rearrange("p (k n) -> p k n", k=KC),
                                     ACT.Copy).then_inc(a_xhi, 1)

            def hidden(h, j):
                n = h * FC + j
                act.wait_ge(p_f1, n + 1)
                if n == 0:
                    act.wait_ge(d_b1, 16)
                if n >= NHB:
                    act.wait_ge(v_hl, n - NHB + 1)
                nc.scalar.activation(hr[:, n % NHB, :], pswt[n % 2][:, 0:RH], ACT.Relu, bias=b1c[:, j:j + 1]).then_inc(a_hr, 1)

            def result(g):
                for b in range(2):
                    act.wait_ge(p_out, g * BG + b + 1)
                    ins = nc.scalar.activation(osb[:, g, b, :], psg[b][:, 0:D], ACT.Copy)
                ins.then_inc(a_out, 1)

            act.wait_ge(v_cpos, 1)
            nc.scalar.activation(lnc0[:], cpos[:], ACT.Ln).then_inc(a_ln, 1)
            abs_sum(0, 0)
            abs_sum(1, 0)
            max_out(0)
            max_out(1)
            exps(0)
            exps(1)
            for u in range(4):
                weights_out(u)
            ctx_out(0)
            ctx_out(1)
            x_hi(0)
            x_hi(1)
            for u in range(4, 8):
                weights_out(u)
            hidden(0, 0)
            max_out(2)
            max_out(3)
            hidden(0, 1)
            exps(2)
            hidden(0, 2)
            exps(3)
            hidden(0, 3)
            hidden(0, 4)
            ctx_out(2)
            ctx_out(3)
            hidden(0, 5)
            hidden(0, 6)
            x_hi(2)
            x_hi(3)
            hidden(0, 7)
            for j in range(4):
                hidden(1, j)
            result(0)
            hidden(1, 4)
            hidden(1, 5)
            result(1)
            hidden(1, 6)
            hidden(1, 7)
            result(2)
            result(3)

        @block.vector
        def _(dve):
            V = nc.vector
            dve.wait_ge(c_iota, 1)
            V.tensor_scalar(pint[:, 0:1], pidx[:], L - 1, None, ALU.bitwise_and).then_inc(c_mod, 1)
            V.tensor_scalar(pint[:, 1:2], pidx[:], 4, KV - 1, ALU.logical_shift_right, ALU.bitwise_and).then_inc(c_mod, 1)
            V.tensor_scalar(pint[:, 2:3], pidx[:], 5, None, ALU.logical_shift_right).then_inc(c_mod, 1)
            dve.wait_ge(c_iota, 2)
            V.tensor_scalar(identf[:], ridx[:], float(P), None, ALU.is_equal).then_inc(c_ident, 1)
            V.tensor_scalar(identb[:], ridx[:], float(P), None, ALU.is_equal).then_inc(c_ident, 1)
            V.tensor_scalar(nidentb[:], ridx[:], float(P), -1.0, ALU.is_equal, ALU.mult).then_inc(c_ident, 1)
            V.tensor_scalar(rmod[:], ridx[:], L - 1, None, ALU.bitwise_and).then_inc(c_mod, 1)
            dve.wait_ge(c_mod, 4)
            V.tensor_copy(pnum[:], pint[:]).then_inc(c_pnum, 1)
            V.tensor_scalar(rep[:], rmod[:], 0.0, None, ALU.is_equal).then_inc(c_rep, 1)
            dve.wait_ge(c_pnum, 1)
            dve.wait_ge(c_iota, 3)
            heads = jdx[:].rearrange("p (n l) -> p n l", l=L)[:, 0:KV, 0]
            V.tensor_scalar(selb[:], jdx[0:B, :], pnum[0:B, 0:1], None, ALU.is_equal).then_inc(c_sel, 1)
            V.tensor_scalar(sel4[:], jdx[0:64, :], pnum[0:64, 0:1], -1.0, ALU.is_equal, ALU.mult).then_inc(c_sel, 1)
            V.tensor_scalar(km[:], heads, pnum[:, 1:2], None, ALU.is_equal).then_inc(c_bm, 1)
            V.tensor_scalar(bm[:], heads, pnum[:, 2:3], None, ALU.is_equal).then_inc(c_bm, 1)
            steps = [0]

            def link(ins):
                steps[0] += 1
                ins.then_inc(v_delta, 1)
                dve.wait_ge(v_delta, steps[0])

            dve.wait_ge(d_tok, 16)
            link(V.tensor_scalar(cmp[:, 0, :], tok[:], float(OPEN_TOKENS[0]), None, ALU.is_equal))
            link(V.scalar_tensor_tensor(cmp[:, 1, :], tok[:], float(OPEN_TOKENS[1]), cmp[:, 0, :], ALU.is_equal, ALU.add))
            link(V.scalar_tensor_tensor(cmp[:, 2, :], tok[:], float(OPEN_TOKENS[2]), cmp[:, 1, :], ALU.is_equal, ALU.add))
            link(V.scalar_tensor_tensor(cmp[:, 3, :], tok[:], float(CLOSE_TOKENS[0]), cmp[:, 2, :], ALU.is_equal, ALU.subtract))
            link(V.scalar_tensor_tensor(cmp[:, 4, :], tok[:], float(CLOSE_TOKENS[1]), cmp[:, 3, :], ALU.is_equal, ALU.add))
            dve.wait_ge(c_scan, 3)
            link(V.scalar_tensor_tensor(sc0[:].rearrange("b (s e) -> b s e", e=2)[:, :, 0], tok[:], float(CLOSE_TOKENS[2]),
                                        cmp[:, 4, :], ALU.is_equal, ALU.add))
            V.tensor_tensor_scan(lev[:], sc0[:], sc1[:], 0.0, ALU.subtract, ALU.max).then_inc(v_lev, 1)

            dve.wait_ge(d_emb, 16)
            V.tensor_scalar(h0[:], emb4[:], EMB_SCALE, None, ALU.mult).then_inc(v_h0, 1)
            dve.wait_ge(v_h0, 1)
            V.bn_stats(st1[:], h0[:]).then_inc(v_st1, 1)
            dve.wait_ge(v_st1, 1)
            V.bn_aggr(mv1[:], st1[:]).then_inc(v_mv1, 1)
            dve.wait_ge(v_mv1, 1)
            V.tensor_scalar(ve1[:], mv1[:, 1:2], EPS, None, ALU.add).then_inc(v_ve1, 1)
            dve.wait_ge(g_rs1, 1)
            V.tensor_scalar(xn1[:], h0[:], mv1[:, 0:1], rs1[:, 0:1], ALU.subtract, ALU.mult).then_inc(v_xn1, 1)
            dve.wait_ge(p_lev, 1)
            V.tensor_scalar(oh[:].rearrange("p g s -> p (g s)"), psmisc[1][:, :], pnum[:, 0:1], None, ALU.is_equal).then_inc(v_oh, 1)
            dve.wait_ge(v_oh, 1)
            V.tensor_reduce(cnt[:], oh[:].bitcast(F32), AX_X, ALU.add).then_inc(v_cnt, 1)
            dve.wait_ge(v_cnt, 1)
            V.tensor_scalar(neg[:], cnt[:], 0.5, ABSENT, ALU.is_lt, ALU.mult).then_inc(v_neg, 1)
            dve.wait_ge(c_bm, 2)
            V.tensor_tensor(cb[:], cnt[:].unsqueeze(2).to_broadcast([P, NG, BG]),
                            bm[:].unsqueeze(1).to_broadcast([P, NG, BG]), ALU.mult).then_inc(v_cb, 1)

            dve.wait_ge(p_k, 1)
            V.scalar_tensor_tensor(ktm[:].rearrange("p (k l) -> p k l", k=KV),
                                   psmisc[1][:, 0:L].unsqueeze(1).to_broadcast([P, KV, L]), SCALE,
                                   km[:].unsqueeze(2).to_broadcast([P, KV, L]), ALU.mult, ALU.mult).then_inc(v_ktm, 1)
            dve.wait_ge(v_ktm, 1)
            V.tensor_copy(khi[:], ktm[:]).then_inc(v_khi, 1)
            dve.wait_ge(v_khi, 1)
            V.tensor_tensor(klo[:], ktm[:], khi[:].bitcast(F32), ALU.subtract).then_inc(v_klo, 1)
            dve.wait_ge(p_q, 1)
            V.tensor_copy(qs[:], psmisc[1][:, P:2 * P]).then_inc(v_qhi, 1)
            dve.wait_ge(v_qhi, 1)
            V.tensor_tensor(qs[64:P, :], psmisc[1][64:P, P:2 * P], qs[64:P, :].bitcast(F32), ALU.subtract).then_inc(v_qs, 1)
            dve.wait_ge(p_v, 1)
            V.tensor_tensor(vo[:, 0:KVD].rearrange("p (k d) -> p k d", k=KV),
                            psmisc[1][:, 2 * P:2 * P + KVD].rearrange("p (k d) -> p k d", k=KV),
                            bm[:].unsqueeze(2).to_broadcast([P, KV, HD]), ALU.mult).then_inc(v_vo, 1)
            V.tensor_copy(vo[:, KVD:VW], bm[:]).then_inc(v_vo, 1)
            dve.wait_ge(p_cnt, 1)
            V.tensor_scalar(cpos[:], psmisc[0][:, 0:B], 1.0, None, ALU.max).then_inc(v_cpos, 1)
            V.tensor_scalar(cabs[:], psmisc[0][:, 0:B], 0.5, ABSENT, ALU.is_lt, ALU.mult).then_inc(v_cpos, 1)

            def abs_sum(w):
                src = w1[:, 0:FC // 2, :].rearrange("p j d -> p (j d)") if w == 0 else w2[:, 0, :]
                dve.wait_ge((d_w1, d_w2)[w][0], 16)
                V.tensor_reduce(asum[:, 2 * w:2 * w + 1], src, AX_X, ALU.add, apply_absolute_value=True).then_inc(v_abs, 1)

            def thresholds(w):
                dve.wait_ge(p_gam[w], 1)
                for i, s in enumerate((1.0, -1.0)):
                    V.tensor_scalar(thr[:, 2 * w + i:2 * w + i + 1], psmisc[w][:, 500:501], s * 0.5 / (D * F), s * 0.5 * EPS,
                                    ALU.mult, ALU.add).then_inc(v_thr, 1)

            def ternary(w, q):
                if q == 0:
                    dve.wait_ge(v_thr, 2 * w + 2)
                flat = w1[:].rearrange("p j d -> p (j d)") if w == 0 else w2[:].rearrange("p c f -> p (c f)")
                if q == 0:
                    dve.wait_ge((d_w1, d_w2)[w][1], 16)
                c = slice(512 * q, 512 * q + 512)
                V.tensor_scalar(tpos[:, w, c], flat[:, c], thr[:, 2 * w:2 * w + 1], None, ALU.is_gt).then_inc(v_tern, 1)
                V.tensor_scalar(tneg[:, w, c], flat[:, c], thr[:, 2 * w + 1:2 * w + 2], None, ALU.is_lt).then_inc(v_tern, 1)

            def maxima(g):
                dve.wait_ge(p_s, g + 1)
                if g == 0:
                    dve.wait_ge(c_misc, 2)
                V.tensor_reduce(mx[:, g, :], psg[g][:, :].rearrange("p (n l) -> p n l", l=L), AX_X, ALU.max).then_inc(v_mx, 1)

                dve.wait_ge(v_mx, g + 1)
                V.tensor_copy(mxr[:, g, 0:GB], mx[:, g, :]).then_inc(v_mhi, 1)
                dve.wait_ge(v_mhi, g + 1)
                V.tensor_tensor(mxr[:, g, 32:32 + GB], mx[:, g, :], mxr[:, g, 0:GB].bitcast(F32), ALU.subtract).then_inc(v_mlo, 1)

            def normalise(g):
                dve.wait_ge(p_ctx, g + 1)
                src = psg[g][:, 0:BG * VW].rearrange("p (b v) -> p b v", b=BG)
                V.reciprocal(rec[:, g, :].rearrange("p (b k) -> p b k", b=BG), src[:, :, KVD:VW]).then_inc(v_rec, 1)
                dve.wait_ge(v_rec, g + 1)
                V.tensor_tensor(cn[:, g, :].rearrange("p (b k d) -> p b k d", b=BG, k=KV),
                                src[:, :, 0:KVD].rearrange("p b (k d) -> p b k d", k=KV),
                                rec[:, g, :].rearrange("p (b k) -> p b k", b=BG).unsqueeze(3).to_broadcast([P, BG, KV, HD]),
                                ALU.mult).then_inc(v_cn, 1)

            def residual_stats(g):
                dve.wait_ge(p_wo, g + 1)
                if g == 0:
                    dve.wait_ge(g_eb, 1)
                V.tensor_tensor(hq[:, g, :], psg[g][:, 0:D], eb[:], ALU.add).then_inc(v_hq, 1)
                dve.wait_ge(v_hq, g + 1)
                V.bn_stats(st2[:, g, :], hq[:, g, :]).then_inc(v_st2, 1)
                dve.wait_ge(v_st2, g + 1)
                V.bn_aggr(mv2[:, g, :], st2[:, g, :]).then_inc(v_mv2, 1)
                dve.wait_ge(v_mv2, g + 1)
                V.tensor_scalar(ve2[:, g:g + 1], mv2[:, g, 1:2], EPS, None, ALU.add).then_inc(v_ve2, 1)

            def norm_rows(g):
                dve.wait_ge(g_rs2, g + 1)
                V.tensor_scalar(xn2[:, g, :], hq[:, g, :], mv2[:, g, 0:1], rs2[:, g:g + 1], ALU.subtract, ALU.mult).then_inc(v_xn2, 1)

            def x_lo(g):
                dve.wait_ge(a_xhi, g + 1)
                V.tensor_tensor(xlo[:, :, g, :], psg[g][:, 0:KC * P].rearrange("p (k n) -> p k n", k=KC),
                                xhi[:, :, g, :].bitcast(F32), ALU.subtract).then_inc(v_xlo, 1)

            def hidden_split(h, j):
                n = h * FC + j
                dve.wait_ge(a_hr, n + 1)
                if n >= NHB:
                    dve.wait_ge(p_f2, n - NHB + 1)
                V.tensor_copy(hh[:, n % NHB, :], hr[:, n % NHB, :]).then_inc(v_hh, 1)
                dve.wait_ge(v_hh, n + 1)
                V.tensor_tensor(hl[:, n % NHB, :], hr[:, n % NHB, :], hh[:, n % NHB, :].bitcast(F32), ALU.subtract).then_inc(v_hl, 1)

            def final_rows(g):
                if g % HALF == 0:
                    dve.wait_ge(p_acc, g // HALF + 1)
                else:
                    dve.wait_ge(p_f2, FC * (g // HALF + 1))
                dve.wait_ge(g_hb, g + 1)
                V.tensor_tensor(fin[:, g, :], psmisc[g % 2][:, 0:D], hb[:, g, :], ALU.add).then_inc(v_fin, 1)
                dve.wait_ge(v_fin, g + 1)
                V.tensor_copy(fhi[:, g, :], fin[:, g, :]).then_inc(v_fhi, 1)
                dve.wait_ge(v_fhi, g + 1)
                V.tensor_tensor(flo[:, g, :], fin[:, g, :], fhi[:, g, :].bitcast(F32), ALU.subtract).then_inc(v_flo, 1)

            def result(g):
                for b in range(2, BG):
                    dve.wait_ge(p_out, g * BG + b + 1)
                    ins = V.tensor_copy(osb[:, g, b, :], psg[b][:, 0:D])
                ins.then_inc(v_out, 1)

            maxima(0)
            maxima(1)
            dve.wait_ge(a_ln, 1)
            dve.wait_ge(v_cpos, 2)
            V.tensor_tensor(lnc[:], lnc0[:], cabs[:], ALU.add).then_inc(v_lnc, 1)
            abs_sum(0)
            thresholds(0)
            for q in range(2):
                ternary(0, q)
            normalise(0)
            normalise(1)
            for q in range(2, 4):
                ternary(0, q)
            residual_stats(0)
            residual_stats(1)
            norm_rows(0)
            norm_rows(1)
            maxima(2)
            maxima(3)
            abs_sum(1)
            x_lo(0)
            x_lo(1)
            thresholds(1)
            for q in range(4):
                ternary(1, q)
            hidden_split(0, 0)
            hidden_split(0, 1)
            hidden_split(0, 2)
            normalise(2)
            hidden_split(0, 3)
            normalise(3)
            hidden_split(0, 4)
            residual_stats(2)
            residual_stats(3)
            hidden_split(0, 5)
            norm_rows(2)
            norm_rows(3)
            hidden_split(0, 6)
            x_lo(2)
            x_lo(3)
            hidden_split(0, 7)
            hidden_split(1, 0)
            final_rows(0)
            final_rows(1)
            for j in range(1, 4):
                hidden_split(1, j)
            result(0)
            hidden_split(1, 4)
            hidden_split(1, 5)
            result(1)
            hidden_split(1, 6)
            hidden_split(1, 7)
            final_rows(2)
            final_rows(3)
            result(2)
            result(3)

        @block.tensor
        def _(pe):
            mm = nc.tensor.matmul
            pe.wait_ge(v_xn1, 1)
            pe.wait_ge(c_ident, 3)
            for k in range(KC):
                ins = nc.tensor.transpose(psmisc[0][:, k * P:(k + 1) * P], xn1[:, k * P:(k + 1) * P], identf[:])
            ins.then_inc(p_xT1, 1)
            pe.wait_ge(v_lev, 1)
            pe.wait_ge(c_sel, 1)
            levels = lev[:].rearrange("b (s e) -> b s e", e=2)[:, :, 1]
            for g in range(NG):
                ins = mm(psmisc[1][:, g * S:(g + 1) * S], selb[:, g * P:(g + 1) * P], levels, start=True, stop=True)
            ins.then_inc(p_lev, 1)

            pe.wait_ge(v_oh, 1)
            pe.wait_ge(a_xT1, 1)
            pe.wait_ge(c_ones, 1)
            pe.wait_ge(d_wk, 32)
            pe.wait_ge(d_bk, 16)
            for k in range(KC):
                mm(psmisc[1][:, 0:L], wk[:, k].rearrange("p r n -> p (r n)"), xT1[:, k, 0:L], start=(k == 0), stop=False)
            mm(psmisc[1][:, 0:L], bkr[:].rearrange("p r n -> p (r n)"), ones[0:1, 0:L], start=False, stop=True).then_inc(p_k, 1)
            pe.wait_ge(g_wqh, 2)
            pe.wait_ge(a_wqh, 2)
            pe.wait_ge(g_bqr, 2)
            pe.wait_ge(v_ktm, 1)
            for h in range(G):
                dst = psmisc[1][:, P + h * L:P + (h + 1) * L]
                for k in range(KC):
                    mm(dst, wqh[:, k, h].rearrange("p r n -> p (r n)"), xT1[:, k, 0:L], start=(k == 0), stop=False)
                ins = mm(dst, bqr[:, h].rearrange("p r n -> p (r n)"), ones[0:1, 0:L], start=False, stop=True)
            ins.then_inc(p_q, 1)
            pe.wait_ge(d_wv, 16)
            pe.wait_ge(d_bv, 16)
            pe.wait_ge(v_qs, 1)
            dst = psmisc[1][:, 2 * P:2 * P + KVD]
            for k in range(KC):
                mm(dst, xT1[:, k, :], wv[:, k, :], start=(k == 0), stop=False)
            mm(dst, ones[0:1, :], bvr[:], start=False, stop=True).then_inc(p_v, 1)
            pe.wait_ge(v_cb, 1)
            pe.wait_ge(c_rep, 1)
            mm(psmisc[0][:, 0:B], rep[:], cb[:].rearrange("p g b -> p (g b)"), start=True, stop=True).then_inc(p_cnt, 1)

            def scores(g):
                if g == 0:
                    pe.wait_ge(v_qs, 1)
                    pe.wait_ge(v_klo, 1)
                    pe.wait_ge(v_neg, 1)
                mm(psg[g][:, :], qs[:], khi[:].unsqueeze(1).to_broadcast([P, BG, P]), start=True, stop=False)
                mm(psg[g][:, :], qs[:], klo[:].unsqueeze(1).to_broadcast([P, BG, P]), start=False, stop=False)
                mm(psg[g][:, :], neg[:, g:g + 1].to_broadcast([P, P]),
                   identb[:].rearrange("p (b l) -> p b l", b=BG).unsqueeze(2).to_broadcast([P, BG, KV, L]),
                   start=False, stop=True).then_inc(p_s, 1)

            def max_t(g):
                pe.wait_ge(v_mlo, g + 1)
                if g >= 2:
                    pe.wait_ge(a_ms, g - 1)
                else:
                    pe.wait_ge(v_cpos, 2)
                    pe.wait_ge(v_vo, 1)
                nc.tensor.transpose(psmisc[g % 2][0:64, 0:P], mxr[:, g, :].bitcast(F32),
                                    identf[:]).then_inc(p_mt, 1)

            def exponents(g):
                rhs = qs[:].unsqueeze(1).to_broadcast([P, BG, P])
                mm(psg[g][:, :], khi[:], rhs, start=True, stop=False)
                mm(psg[g][:, :], klo[:], rhs, start=False, stop=True)
                pe.wait_ge(a_ms, g + 1)
                pe.wait_ge(c_sel, 2)
                for b in range(BG):
                    ins = mm(psg[g][:, b * P:(b + 1) * P], sel4[:, b * P:(b + 1) * P], ms[:, g, :], start=False, stop=True,
                             skip_group_check=True)
                ins.then_inc(p_et, 1)

            def context(g):
                pe.wait_ge(v_vo, 2)
                pe.wait_ge(a_exp, BG * (g + 1))
                for b in range(BG):
                    ins = mm(psg[g][:, b * VW:(b + 1) * VW], et[:, g, b, :], vo[:], start=True, stop=True)
                ins.then_inc(p_ctx, 1)

            def context_t(g):
                pe.wait_ge(v_cn, g + 1)
                for b in range(BG):
                    ins = nc.tensor.transpose(psg[g][0:64, b * P:(b + 1) * P], cn[:, g, b * KVD:(b + 1) * KVD], identf[:])
                ins.then_inc(p_cT, 1)

            def out_proj(g):
                pe.wait_ge(a_cT, 2 * (g + 1))
                if g == 0:
                    for i in range(4):
                        pe.wait_ge(d_wo[i], 16)
                for e in range(H2):
                    ins = mm(psg[g][:, 0:D], cT[:, g, e].rearrange("p b l -> p (b l)"), wo[:, e, :], start=(e == 0), stop=(e == H2 - 1))
                ins.then_inc(p_wo, 1)

            def rows_t(g):
                pe.wait_ge(v_xn2, g + 1)
                for k in range(KC):
                    ins = nc.tensor.transpose(psg[g][:, k * P:(k + 1) * P], xn2[:, g, k * P:(k + 1) * P], identf[:])
                ins.then_inc(p_xT2, 1)

            def abs_total(w):
                pe.wait_ge(v_abs, w + 1)
                pe.wait_ge(a_abs, w + 1)
                if w == 0:
                    pe.wait_ge(a_ms, 1)
                for i in range(2):
                    ins = mm(psmisc[w][:, 500:501], ones[:], asum[:, 2 * w + i:2 * w + i + 1], start=(i == 0), stop=(i == 1))
                ins.then_inc(p_gam[w], 1)

            def weights_t(u):
                w, i = divmod(u, 4)
                if w == 0:
                    pe.wait_ge(v_tern, 2 * (i + 1))
                else:
                    pe.wait_ge(v_tern, 16)
                if u >= 2:
                    pe.wait_ge(a_wt, u - 1)
                for jj in range(2):
                    for k in range(KC):
                        j = 2 * i + jj
                        dst = pswt[u % 2][:, (jj * KC + k) * P:(jj * KC + k + 1) * P]
                        for n, (t, idn) in enumerate(((tpos, identb), (tneg, nidentb))):
                            if w == 0:
                                src = t[:, 0, j * D + k * P:j * D + (k + 1) * P]
                            else:
                                src = t[:, 1, k * F:(k + 1) * F].rearrange("p (f j) -> p j f", j=FC)[:, j]
                            ins = mm(dst, src, idn[:], start=(n == 0), stop=(n == 1))
                ins.then_inc(p_wt, 1)

            def ffn1(h, j):
                n = h * FC + j
                if n == 0:
                    pe.wait_ge(a_wt, 8)
                if j == 0:
                    pe.wait_ge(v_xlo, HALF * (h + 1))
                if n >= 2:
                    pe.wait_ge(a_hr, n - 1)
                for m, part in enumerate((xhi, xlo)):
                    for k in range(KC):
                        ins = mm(pswt[n % 2][:, 0:RH], w1T[:, j, k, :], part[:, k, HALF * h:HALF * (h + 1), :].rearrange("p g n -> p (g n)"),
                                 start=(m == 0 and k == 0), stop=(m == 1 and k == KC - 1))
                ins.then_inc(p_f1, 1)

            def ffn2(h, j):
                n = h * FC + j
                pe.wait_ge(v_hl, n + 1)
                if j == 0:
                    if h == 0:
                        pe.wait_ge(a_ms, 4)
                        pe.wait_ge(v_thr, 4)
                    else:
                        pe.wait_ge(v_fin, 2)
                for r in range(HALF):
                    for m, part in enumerate((hh, hl)):
                        ins = mm(psmisc[r][:, 0:D], part[:, n % NHB, r * P:(r + 1) * P], w2T[:, j, :],
                                 start=(j == 0 and m == 0), stop=(j == FC - 1 and m == 1))
                    if j == FC - 1 and r == 0:
                        ins.then_inc(p_acc, 1)
                ins.then_inc(p_f2, 1)

            def spread(g):
                pe.wait_ge(v_flo, g + 1)
                if g == 0:
                    pe.wait_ge(v_xlo, NG)
                for b in range(BG):
                    if g > 0:
                        pe.wait_ge((a_out, v_out)[b // 2], g)
                    q = slice(L * b, L * (b + 1))
                    mm(psg[b][:, 0:D], oh[q, g, :], fhi[q, g, :], start=True, stop=False)
                    mm(psg[b][:, 0:D], oh[q, g, :], flo[q, g, :], start=False, stop=True).then_inc(p_out, 1)

            for g in range(NG):
                scores(g)
            max_t(0)
            max_t(1)
            exponents(0)
            exponents(1)
            context(0)
            context(1)
            abs_total(0)
            for u in range(2):
                weights_t(u)
            context_t(0)
            context_t(1)
            for u in range(2, 4):
                weights_t(u)
            out_proj(0)
            out_proj(1)
            abs_total(1)
            rows_t(0)
            rows_t(1)
            for u in range(4, 8):
                weights_t(u)
            ffn1(0, 0)
            max_t(2)
            max_t(3)
            ffn1(0, 1)
            exponents(2)
            exponents(3)
            ffn2(0, 0)
            ffn1(0, 2)
            context(2)
            ffn2(0, 1)
            ffn1(0, 3)
            context(3)
            ffn2(0, 2)
            ffn1(0, 4)
            context_t(2)
            context_t(3)
            ffn2(0, 3)
            ffn1(0, 5)
            out_proj(2)
            out_proj(3)
            ffn2(0, 4)
            ffn1(0, 6)
            ffn2(0, 5)
            rows_t(2)
            rows_t(3)
            ffn1(0, 7)
            ffn2(0, 6)
            ffn1(1, 0)
            ffn2(0, 7)
            for j in range(1, 4):
                ffn1(1, j)
                ffn2(1, j - 1)
            spread(0)
            for j in range(4, 6):
                ffn1(1, j)
                ffn2(1, j - 1)
            spread(1)
            for j in range(6, FC):
                ffn1(1, j)
                ffn2(1, j - 1)
            ffn2(1, FC - 1)
            spread(2)
            spread(3)


_INS = ["x", "L0_tok_level_emb", "L0_attn_Wq", "L0_attn_bq", "L0_attn_Wk", "L0_attn_bk", "L0_attn_Wv", "L0_attn_bv",
        "L0_attn_Wo", "L0_attn_bo", "L0_ffn_W1", "L0_ffn_b1", "L0_ffn_W2", "L0_ffn_b2"]


def kernel(**inputs):
    import numpy as _np
    import concourse.bacc as _bacc
    from concourse import mybir as _mybir
    from concourse.bass_utils import run_bass_kernel_spmd as _run

    nc = _bacc.Bacc("TRN2", target_bir_lowering=False, num_devices=1)
    arrays, args = {}, []
    for name in _INS:
        a = _np.ascontiguousarray(inputs[name])
        arrays[f"in_{name}_dram"] = a
        args.append(nc.dram_tensor(f"in_{name}_dram", a.shape, _mybir.dt.from_np(a.dtype), kind="ExternalInput").ap())
    shape = tuple(inputs["x"].shape) + (inputs["L0_tok_level_emb"].shape[1],)
    args.append(nc.dram_tensor("out_0_dram", shape, _mybir.dt.float32, kind="ExternalOutput").ap())
    level_tower(nc, *args)
    r = _run(nc, [arrays], core_ids=[0])
    return r.results[0]["out_0_dram"]
```

```python
from contextlib import ExitStack

import concourse.bass as bass
from concourse import mybir

F32 = mybir.dt.float32
F32R = mybir.dt.float32r
BF16 = mybir.dt.bfloat16
I32 = mybir.dt.int32
ALU = mybir.AluOpType
ACT = mybir.ActivationFunctionType
AX_X = mybir.AxisListType.X

P = 128
OPEN_TOKENS = (40, 91, 123)
CLOSE_TOKENS = (41, 93, 125)
EMB_SCALE = 0.15
EPS = 1e-5
ABSENT = -1e30


def level_tower(nc, x, emb, Wq, bq, Wk, bk, Wv, bv, Wo, bo, W1, b1, W2, b2, out):
    B, S = x.shape
    L, D = emb.shape
    KVD = Wk.shape[1]
    HD = 16
    KV = KVD // HD
    G = D // HD // KV
    F = W1.shape[0]
    KC = D // P
    FC = F // P
    BG = P // L
    NG = B // BG
    HALF = NG // 2
    H2 = G // 2
    GB = BG * KV
    RH = HALF * P
    VW = KVD + KV
    SCALE = float(HD) ** -0.5
    assert S == P and L == 32 and D == 2 * P and G == 4 and KV == 4 and NG == 4 and F % P == 0

    ctx = ExitStack()
    with ctx:
        def sb(name, shape, dt=F32):
            return ctx.enter_context(nc.sbuf_tensor(name, shape, dt))

        def sem(name):
            return ctx.enter_context(nc.semaphore(name))

        pswt = [ctx.enter_context(nc.psum_tensor(f"pswt{i}", [P, 512], F32)) for i in range(2)]
        psmisc = [ctx.enter_context(nc.psum_tensor(f"psmisc{i}", [P, 512], F32)) for i in range(2)]
        psg = [ctx.enter_context(nc.psum_tensor(f"psg{i}", [P, 512], F32)) for i in range(NG)]

        tok = sb("tok", [B, S], I32)
        emb4 = sb("emb4", [P, D])
        wq = sb("wq", [P, KC, D])
        wqh = sb("wqh", [P, KC, G, KVD])
        wk1 = sb("wk1", [P, KC, KVD])
        bk1 = sb("bk1", [1, KVD])
        wk = sb("wk", [P, KC, 2, KVD])
        wv = sb("wv", [P, KC, KVD])
        brow = sb("brow", [1, D])
        bqr = sb("bqr", [1, G, KVD])
        bkr = sb("bkr", [1, 2, KVD])
        bvr = sb("bvr", [1, KVD])
        wo = sb("wo", [P, H2, D])
        bo_bc = sb("bo_bc", [P, D])
        b2_bc = sb("b2_bc", [P, D])
        b1c = sb("b1c", [P, FC])
        w1 = sb("w1", [P, FC, D])
        w2 = sb("w2", [P, KC, F])
        identf = sb("identf", [P, P])
        ident2 = sb("ident2", [P, P], BF16)
        identr = sb("identr", [P, P], F32R)
        identb = sb("identb", [P, P], BF16)
        ones = sb("ones", [P, P])
        sel4 = sb("sel4", [64, 512], F32R)
        selb = sb("selb", [B, 512], BF16)
        bm = sb("bm", [P, BG])
        km = sb("km", [P, KV])
        pidx = sb("pidx", [P, 1], I32)
        pint = sb("pint", [P, 3], I32)
        pnum = sb("pnum", [P, 3])
        ridx = sb("ridx", [P, P], I32)
        rmod = sb("rmod", [P, P], I32)
        jdx = sb("jdx", [P, GB], I32)
        warm = sb("warm", [P, 512], BF16)
        tiny = sb("tiny", [1, 2])
        rep = sb("rep", [P, P], BF16)
        mhalf = sb("mhalf", [P, 1])
        cmp = sb("cmp", [B, 7, S])
        sc0 = sb("sc0", [B, 2 * S])
        sc1 = sb("sc1", [B, 2 * S])
        lev = sb("lev", [B, 2 * S], BF16)
        oh = sb("oh", [P, NG, S], F32R)
        cnt = sb("cnt", [P, NG])
        neg = sb("neg", [P, NG], BF16)
        cb = sb("cb", [P, NG, BG], BF16)
        cpos = sb("cpos", [P, B])
        cabs = sb("cabs", [P, B])
        st1 = sb("st1", [P, 6])
        mv1 = sb("mv1", [P, 2])
        ve1 = sb("ve1", [P, 1])
        rs1 = sb("rs1", [P, 1])
        xn1 = sb("xn1", [P, D])
        xT1 = sb("xT1", [P, KC, P])
        qs = sb("qs", [P, P], F32R)
        ktm = sb("ktm", [P, P])
        khi = sb("khi", [P, P], F32R)
        klo = sb("klo", [P, P], F32R)
        vo = sb("vo", [P, VW])
        voc = sb("voc", [P, B, VW])
        eb = sb("eb", [P, D])
        mx = sb("mx", [P, NG, GB])
        mxr = sb("mxr", [P, NG, 64], F32R)
        ms = sb("ms", [64, NG, P], F32R)
        et = sb("et", [P, NG, BG, P])
        rec = sb("rec", [P, NG, GB])
        cn = sb("cn", [P, NG, BG * KVD])
        cT = sb("cT", [P, NG, H2, BG, L])
        hq = sb("hq", [P, NG, D])
        hb = sb("hb", [P, NG, D])
        hbh = sb("hbh", [P, NG, D], F32R)
        hbl = sb("hbl", [P, NG, D], F32R)
        st2 = sb("st2", [P, NG, 6])
        mv2 = sb("mv2", [P, NG, 2])
        ve2 = sb("ve2", [P, NG])
        rs2 = sb("rs2", [P, NG])
        xn2 = sb("xn2", [P, NG, D])
        xhi = sb("xhi", [P, KC, NG, P], F32R)
        xlo = sb("xlo", [P, KC, NG, P], F32R)
        asum = sb("asum", [P, 4])
        thr = sb("thr", [P, 2])
        aw = sb("aw", [P, 2, 2048])
        sg = sb("sg", [P, 2, 2048], BF16)
        tern = sb("tern", [P, 2, 2048], BF16)
        w1T = sb("w1T", [P, FC, KC, P], F32R)
        w2T = sb("w2T", [P, FC, D], F32R)
        NHR = 4
        NH = 2 * FC
        hr = sb("hr", [P, NHR, RH])
        hh = sb("hh", [P, NH, RH], F32R)
        hl = sb("hl", [P, NH, RH], F32R)
        fhi = sb("fhi", [P, NG, D], F32R)
        flo = sb("flo", [P, NG, D], F32R)
        osb = aw[:].rearrange("p w n -> p (w n)").rearrange("p (g b d) -> p g b d", g=NG, b=BG)

        d_tok, d_emb, d_wq, d_wk, d_wv, d_bq, d_bk, d_bv = (sem("d_" + n) for n in "tok emb wq wk wv bq bk bv".split())
        d_bo, d_b1, d_b2 = (sem("d_" + n) for n in "bo b1 b2".split())
        d_w1 = [sem(f"d_w1_{i}") for i in range(2)]
        d_w2 = [sem(f"d_w2_{i}") for i in range(2)]
        d_wo = [sem(f"d_wo_{i}") for i in range(4)]
        d_out = sem("d_out")

        c_ones = sem("c_ones")
        c_iota = sem("c_iota")
        c_misc = sem("c_misc")
        c_pnum = sem("c_pnum")
        c_ident = sem("c_ident")
        c_sel = sem("c_sel")
        c_bm = sem("c_bm")
        c_mod = sem("c_mod")
        c_rep = sem("c_rep")
        c_scan = sem("c_scan")
        v_warm = sem("v_warm")
        a_table = sem("a_table")
        v_cmp = sem("v_cmp")
        v_pair = sem("v_pair")
        v_sum = sem("v_sum")
        v_lev = sem("v_lev")
        p_lev = sem("p_lev")
        v_oh = sem("v_oh")
        v_cnt = sem("v_cnt")
        v_neg = sem("v_neg")
        v_cb = sem("v_cb")
        p_cnt = sem("p_cnt")
        v_cpos = sem("v_cpos")
        v_st1 = sem("v_st1")
        v_mv1 = sem("v_mv1")
        v_ve1 = sem("v_ve1")
        g_rs1 = sem("g_rs1")
        v_xn1 = sem("v_xn1")
        p_xT1 = sem("p_xT1")
        a_xT1 = sem("a_xT1")
        p_k = sem("p_k")
        p_q = sem("p_q")
        p_v = sem("p_v")
        v_ktm = sem("v_ktm")
        v_khi = sem("v_khi")
        v_klo = sem("v_klo")
        v_qhi = sem("v_qhi")
        v_qs = sem("v_qs")
        v_vo = sem("v_vo")
        v_eb = sem("v_eb")
        g_voc = sem("g_voc")
        a_bqr = sem("a_bqr")
        a_wk = sem("a_wk")
        a_bkr = sem("a_bkr")
        a_wqh = sem("a_wqh")
        p_s = sem("p_s")
        v_mx = sem("v_mx")
        p_mt = sem("p_mt")
        a_ms = sem("a_ms")
        v_mhi = sem("v_mhi")
        v_mlo = sem("v_mlo")
        p_et = sem("p_et")
        a_exp = sem("a_exp")
        p_ctx = sem("p_ctx")
        v_rec = sem("v_rec")
        v_cn = sem("v_cn")
        p_cT = sem("p_cT")
        a_cT = sem("a_cT")
        p_wo = sem("p_wo")
        v_hq = sem("v_hq")
        g_hb = sem("g_hb")
        g_hbh = sem("g_hbh")
        g_hbl = sem("g_hbl")
        v_st2 = sem("v_st2")
        v_mv2 = sem("v_mv2")
        v_ve2 = sem("v_ve2")
        g_rs2 = sem("g_rs2")
        v_xn2 = sem("v_xn2")
        p_xT2 = sem("p_xT2")
        a_xhi = sem("a_xhi")
        v_xlo = sem("v_xlo")
        a_abs = sem("a_abs")
        a_sgn = sem("a_sgn")
        g_sgn = sem("g_sgn")
        p_gam = [sem(f"p_gam{i}") for i in range(2)]
        v_thr = sem("v_thr")
        v_tern = sem("v_tern")
        p_wt = sem("p_wt")
        a_wt = sem("a_wt")
        p_f1 = sem("p_f1")
        a_hr = sem("a_hr")
        a_hh = sem("a_hh")
        v_hl = sem("v_hl")
        p_acc = sem("p_acc")
        a_fhi = sem("a_fhi")
        v_flo = sem("v_flo")
        p_out = sem("p_out")
        a_out = sem("a_out")
        v_out = sem("v_out")

        block = ctx.enter_context(nc.Block())

        w1_rows = W1.rearrange("(p j) d -> p j d", j=FC)
        w2_rows = W2.rearrange("(c p) f -> p c f", p=P)
        wo_rows = Wo.rearrange("(k a e d) n -> a e k d n", k=KV, a=2, e=H2)

        def halves(w, i):
            return w1[:, i * FC // 2:(i + 1) * FC // 2, :].rearrange("p j d -> p (j d)") if w == 0 else w2[:, i, :]

        def out_banks(g):
            return psg if g < NG - 1 else [pswt[0], pswt[1], psmisc[0], psg[0]]

        @block.sync
        def _(sp):
            sp.dma_start(emb4[:], emb.unsqueeze(0).to_broadcast([BG, L, D])).then_inc(d_emb, 16)
            sp.dma_start(wk1[:], Wk.rearrange("(c p) n -> p c n", p=P)).then_inc(d_wk, 16)
            sp.dma_start(wq[:], Wq.rearrange("(c p) n -> p c n", p=P)).then_inc(d_wq, 16)
            sp.dma_start(bk1[:], bk.unsqueeze(0)).then_inc(d_bk, 16)
            sp.dma_start(brow[:], bq.unsqueeze(0)).then_inc(d_bq, 16)
            sp.dma_start(wv[:], Wv.rearrange("(c p) n -> p c n", p=P)).then_inc(d_wv, 16)
            sp.dma_start(bvr[:], bv.unsqueeze(0)).then_inc(d_bv, 16)
            for i in range(2):
                c = slice(i * FC // 2, (i + 1) * FC // 2)
                sp.dma_start(w1[:, c, :], w1_rows[:, c, :]).then_inc(d_w1[i], 16)
            for i in range(2):
                sp.dma_start(w2[:, i, :], w2_rows[:, i, :]).then_inc(d_w2[i], 16)
            for a in range(2):
                for e in range(H2):
                    sp.dma_start(wo[64 * a:64 * a + 64, e, :], wo_rows[a, e]).then_inc(d_wo[2 * a + e], 16)
            sp.dma_start(bo_bc[:], bo.unsqueeze(0).to_broadcast([P, D])).then_inc(d_bo, 16)
            sp.dma_start(b1c[:], b1.rearrange("(p j) -> p j", j=FC)).then_inc(d_b1, 16)
            sp.dma_start(b2_bc[:], b2.unsqueeze(0).to_broadcast([P, D])).then_inc(d_b2, 16)
            out_t = out.rearrange("b s d -> s b d")
            for g in range(NG):
                for e in range(2):
                    if e == 0:
                        sp.wait_ge(a_out, g + 1)
                    else:
                        sp.wait_ge(v_out, g + 1)
                    b0 = g * BG + 2 * e
                    sp.dma_start(out_t[:, b0:b0 + 2, :], osb[:, g, 2 * e:2 * e + 2, :]).then_inc(d_out, 16)
            sp.wait_ge(d_out, 16 * 2 * NG)

        @block.gpsimd
        def _(pool):
            nc.gpsimd.memset(sc0[:], 0.0).then_inc(c_scan, 1)
            nc.gpsimd.memset(sc1[:], 0.0).then_inc(c_scan, 1)
            pool.wait_ge(c_scan, 2)
            nc.gpsimd.memset(sc1[:].rearrange("b (s e) -> b s e", e=2)[:, :, 0:1], float(1 - L)).then_inc(c_scan, 1)
            nc.gpsimd.iota(pidx[:], pattern=[[0, 1]], base=0, channel_multiplier=1).then_inc(c_iota, 1)
            nc.gpsimd.iota(ridx[:], pattern=[[-1, P]], base=P, channel_multiplier=1).then_inc(c_iota, 1)
            nc.gpsimd.iota(jdx[:], pattern=[[1, GB]], base=0, channel_multiplier=0).then_inc(c_iota, 1)
            nc.gpsimd.memset(mhalf[:], -0.5).then_inc(c_misc, 1)
            nc.gpsimd.memset(ones[:], 1.0).then_inc(c_ones, 1)
            pool.wait_ge(v_ve1, 1)
            pool.wait_ge(c_misc, 1)
            nc.gpsimd.tensor_tensor(rs1[:], ve1[:], mhalf[:], ALU.pow).then_inc(g_rs1, 1)
            nc.gpsimd.memset(mxr[:].bitcast(F32), 0.0).then_inc(c_misc, 1)
            pool.wait_ge(v_vo, 2)
            pool.wait_ge(v_cpos, 2)
            for g in range(NG):
                bs = slice(g * BG, (g + 1) * BG)
                nc.gpsimd.tensor_tensor(voc[:, bs, :], vo[:].unsqueeze(1).to_broadcast([P, BG, VW]),
                                        cpos[:, bs].unsqueeze(2).to_broadcast([P, BG, VW]), ALU.mult).then_inc(g_voc, 1)
            for i in range(2):
                pool.wait_ge(d_w2[i], 16)
                nc.gpsimd.tensor_scalar(sg[:, 1, i * 1024:(i + 1) * 1024], halves(1, i), 0.0, 0.5,
                                        ALU.is_ge, ALU.subtract).then_inc(g_sgn, 1)
            pool.wait_ge(d_b2, 16)
            for h in range(NG // HALF):
                gs = range(h * HALF, (h + 1) * HALF)
                c = slice(h * HALF, (h + 1) * HALF)
                pool.wait_ge(v_ve2, (h + 1) * HALF)
                nc.gpsimd.tensor_tensor(rs2[:, c], ve2[:, c], mhalf[:].to_broadcast([P, HALF]), ALU.pow).then_inc(g_rs2, 1)
                for g in gs:
                    nc.gpsimd.tensor_tensor(hb[:, g, :], hq[:, g, :], b2_bc[:], ALU.add).then_inc(g_hb, 1)
                for g in gs:
                    pool.wait_ge(g_hb, g + 1)
                    nc.gpsimd.tensor_copy(hbh[:, g, :], hb[:, g, :]).then_inc(g_hbh, 1)
                for g in gs:
                    pool.wait_ge(g_hbh, g + 1)
                    nc.gpsimd.tensor_tensor(hbl[:, g, :], hb[:, g, :], hbh[:, g, :].bitcast(F32), ALU.subtract).then_inc(g_hbl, 1)

        @block.scalar
        def _(act):
            act.dma_start(tok[:], x).then_inc(d_tok, 16)
            act.wait_ge(v_warm, 2)
            nc.scalar.activation(tiny[0:1, 1:2], tiny[0:1, 0:1], ACT.Exp).then_inc(a_table, 1)
            act.wait_ge(d_wk, 16)
            nc.scalar.activation(wk[:], wk1[:].unsqueeze(2).to_broadcast([P, KC, 2, KVD]), ACT.Copy).then_inc(a_wk, 1)
            act.wait_ge(d_wq, 16)
            for k in range(KC):
                nc.scalar.activation(wqh[:, k].rearrange("p h (k d) -> p h k d", k=KV),
                                     wq[:, k, :].rearrange("p (k h d) -> p h k d", k=KV, h=G), ACT.Copy).then_inc(a_wqh, 1)
            act.wait_ge(d_bk, 16)
            nc.scalar.activation(bkr[:], bk1[:].unsqueeze(1).to_broadcast([1, 2, KVD]), ACT.Copy).then_inc(a_bkr, 1)
            act.wait_ge(p_xT1, 1)
            nc.scalar.activation(xT1[:], psmisc[0][:, 0:KC * P].rearrange("p (k n) -> p k n", k=KC), ACT.Copy).then_inc(a_xT1, 1)
            act.wait_ge(d_bq, 16)
            nc.scalar.activation(bqr[:].rearrange("p h (k d) -> p h k d", k=KV), brow[:].rearrange("p (k h d) -> p h k d", k=KV, h=G),
                                 ACT.Copy).then_inc(a_bqr, 1)

            def magnitudes(w, i):
                act.wait_ge((d_w1, d_w2)[w][i], 16)
                nc.scalar.activation(aw[:, w, i * 1024:(i + 1) * 1024], halves(w, i), ACT.Abs,
                                     accum_out=asum[:, 2 * w + i:2 * w + i + 1]).then_inc(a_abs, 1)

            def signs(i):
                nc.scalar.activation(sg[:, 0, i * 1024:(i + 1) * 1024], halves(0, i), ACT.Sign).then_inc(a_sgn, 1)

            def weights_out(u):
                act.wait_ge(p_wt, u + 1)
                src = (pswt, psg)[u // 4][u % 2][:, :]
                j = 2 * (u % 4)
                if u < 4:
                    nc.scalar.activation(w1T[:, j:j + 2, :, :].rearrange("p j k f -> p (j k f)"), src, ACT.Copy).then_inc(a_wt, 1)
                else:
                    nc.scalar.activation(w2T[:, j:j + 2, :].rearrange("p j d -> p (j d)"), src, ACT.Copy).then_inc(a_wt, 1)

            def max_out(g):
                act.wait_ge(p_mt, g + 1)
                nc.scalar.activation(ms[:, g, :], psmisc[g % 2][0:64, 0:P], ACT.Copy).then_inc(a_ms, 1)

            def exps(g):
                act.wait_ge(p_et, g + 1)
                if g == 0:
                    act.wait_ge(v_cpos, 2)
                for b in range(BG):
                    n = g * BG + b
                    nc.scalar.activation(et[:, g, b, :], psg[g][:, b * P:(b + 1) * P], ACT.Exp,
                                         bias=cabs[:, n:n + 1]).then_inc(a_exp, 1)

            def ctx_out(g):
                act.wait_ge(p_cT, g + 1)
                src = psg[g][0:64, :].rearrange("p (b a e l) -> p a b e l", b=BG, a=2, e=H2)
                for a in range(2):
                    dst = cT[64 * a:64 * a + 64, g].rearrange("p e b l -> p b e l")
                    nc.scalar.activation(dst, src[:, a], ACT.Copy).then_inc(a_cT, 1)

            def x_hi(g):
                act.wait_ge(p_xT2, g + 1)
                nc.scalar.activation(xhi[:, :, g, :], psg[g][:, 0:KC * P].rearrange("p (k n) -> p k n", k=KC),
                                     ACT.Copy).then_inc(a_xhi, 1)

            def hidden(h, j):
                n = h * FC + j
                act.wait_ge(p_f1, n + 1)
                if n == 0:
                    act.wait_ge(d_b1, 16)
                if n >= NHR:
                    act.wait_ge(v_hl, n - NHR + 1)
                nc.scalar.activation(hr[:, n % NHR, :], pswt[n % 2][:, 0:RH], ACT.Relu, bias=b1c[:, j:j + 1]).then_inc(a_hr, 1)
                nc.scalar.activation(hh[:, n, :], pswt[n % 2][:, 0:RH], ACT.Relu, bias=b1c[:, j:j + 1]).then_inc(a_hh, 1)

            def final_hi(g):
                act.wait_ge(p_acc, g + 1)
                nc.scalar.activation(fhi[:, g, :], psmisc[g % 2][:, 0:D], ACT.Copy).then_inc(a_fhi, 1)

            def result(g):
                for b in range(2):
                    act.wait_ge(p_out, g * BG + b + 1)
                    ins = nc.scalar.activation(osb[:, g, b, :], out_banks(g)[b][:, 0:D], ACT.Copy)
                ins.then_inc(a_out, 1)

            magnitudes(0, 0)
            signs(0)
            magnitudes(0, 1)
            magnitudes(1, 0)
            signs(1)
            max_out(0)
            max_out(1)
            max_out(2)
            exps(0)
            exps(1)
            magnitudes(1, 1)
            max_out(3)
            exps(2)
            ctx_out(0)
            ctx_out(1)
            exps(3)
            weights_out(0)
            ctx_out(2)
            ctx_out(3)
            weights_out(1)
            x_hi(0)
            x_hi(1)
            weights_out(2)
            weights_out(3)
            hidden(0, 0)
            hidden(0, 1)
            weights_out(4)
            weights_out(5)
            hidden(0, 2)
            hidden(0, 3)
            weights_out(6)
            hidden(0, 4)
            hidden(0, 5)
            x_hi(2)
            x_hi(3)
            hidden(0, 6)
            hidden(0, 7)
            weights_out(7)
            hidden(1, 0)
            final_hi(0)
            hidden(1, 1)
            final_hi(1)
            hidden(1, 2)
            hidden(1, 3)
            result(0)
            hidden(1, 4)
            hidden(1, 5)
            result(1)
            hidden(1, 6)
            hidden(1, 7)
            final_hi(2)
            final_hi(3)
            result(2)
            result(3)

        @block.vector
        def _(dve):
            V = nc.vector
            V.memset(warm[:], 0.0).then_inc(v_warm, 1)
            V.memset(tiny[:], 0.0).then_inc(v_warm, 1)
            dve.wait_ge(c_iota, 1)
            V.tensor_scalar(pint[:, 0:1], pidx[:], L - 1, None, ALU.bitwise_and).then_inc(c_mod, 1)
            V.tensor_scalar(pint[:, 1:2], pidx[:], 4, KV - 1, ALU.logical_shift_right, ALU.bitwise_and).then_inc(c_mod, 1)
            V.tensor_scalar(pint[:, 2:3], pidx[:], 5, None, ALU.logical_shift_right).then_inc(c_mod, 1)
            dve.wait_ge(c_iota, 2)
            V.tensor_scalar(identf[:], ridx[:], float(P), None, ALU.is_equal).then_inc(c_ident, 1)
            dve.wait_ge(c_mod, 3)
            V.tensor_copy(pnum[:], pint[:]).then_inc(c_pnum, 1)
            dve.wait_ge(c_pnum, 1)
            dve.wait_ge(c_iota, 3)
            V.tensor_scalar(selb[:].rearrange("p (n l) -> p n l", l=L), jdx[0:B, :].unsqueeze(2).to_broadcast([B, GB, L]),
                            pnum[0:B, 0:1], None, ALU.is_equal).then_inc(c_sel, 1)
            dve.wait_ge(d_emb, 16)
            V.bn_stats(st1[:], emb4[:]).then_inc(v_st1, 1)
            dve.wait_ge(d_tok, 16)
            for i, t in enumerate(OPEN_TOKENS):
                V.tensor_scalar(cmp[:, i, :], tok[:], float(t), None, ALU.is_equal).then_inc(v_cmp, 1)
            dve.wait_ge(v_st1, 1)
            V.bn_aggr(mv1[:], st1[:]).then_inc(v_mv1, 1)

            def closing(i, t):
                dve.wait_ge(v_cmp, i + 1)
                V.scalar_tensor_tensor(cmp[:, 3 + i, :], tok[:], float(t), cmp[:, i, :], ALU.is_equal, ALU.subtract).then_inc(v_pair, 1)

            closing(0, CLOSE_TOKENS[0])
            dve.wait_ge(v_mv1, 1)
            V.tensor_scalar(ve1[:], mv1[:, 1:2], EPS / EMB_SCALE ** 2, None, ALU.add).then_inc(v_ve1, 1)
            closing(1, CLOSE_TOKENS[1])
            closing(2, CLOSE_TOKENS[2])
            dve.wait_ge(v_pair, 2)
            V.tensor_tensor(cmp[:, 6, :], cmp[:, 3, :], cmp[:, 4, :], ALU.add).then_inc(v_sum, 1)
            dve.wait_ge(g_rs1, 1)
            V.tensor_scalar(xn1[:], emb4[:], mv1[:, 0:1], rs1[:, 0:1], ALU.subtract, ALU.mult).then_inc(v_xn1, 1)
            dve.wait_ge(v_pair, 3)
            dve.wait_ge(v_sum, 1)
            dve.wait_ge(c_scan, 3)
            V.tensor_tensor(sc0[:].rearrange("b (s e) -> b s e", e=2)[:, :, 0], cmp[:, 6, :], cmp[:, 5, :], ALU.add).then_inc(v_sum, 1)
            dve.wait_ge(v_sum, 2)
            V.tensor_tensor_scan(lev[:], sc0[:], sc1[:], 0.0, ALU.subtract, ALU.max).then_inc(v_lev, 1)
            V.tensor_scalar(km[:], jdx[:, 0:KV], pnum[:, 1:2], None, ALU.is_equal).then_inc(c_bm, 1)
            V.tensor_scalar(bm[:], jdx[:, 0:KV], pnum[:, 2:3], None, ALU.is_equal).then_inc(c_bm, 1)
            V.tensor_scalar(identb[:], ridx[:], float(P), None, ALU.is_equal).then_inc(c_ident, 1)
            V.tensor_scalar(rmod[:], ridx[:], L - 1, None, ALU.bitwise_and).then_inc(c_mod, 1)
            dve.wait_ge(c_mod, 4)
            V.tensor_scalar(rep[:], rmod[:], 0.0, None, ALU.is_equal).then_inc(c_rep, 1)

            dve.wait_ge(p_lev, 1)
            V.tensor_scalar(oh[:].rearrange("p g s -> p (g s)"), pswt[0][:, :], pnum[:, 0:1], None, ALU.is_equal).then_inc(v_oh, 1)
            dve.wait_ge(v_oh, 1)
            V.tensor_reduce(cnt[:], oh[:].bitcast(F32), AX_X, ALU.add).then_inc(v_cnt, 1)
            dve.wait_ge(c_bm, 2)
            dve.wait_ge(p_k, 1)
            V.scalar_tensor_tensor(ktm[:].rearrange("p (k l) -> p k l", k=KV),
                                   psmisc[1][:, 0:L].unsqueeze(1).to_broadcast([P, KV, L]), SCALE,
                                   km[:].unsqueeze(2).to_broadcast([P, KV, L]), ALU.mult, ALU.mult).then_inc(v_ktm, 1)
            dve.wait_ge(v_cnt, 1)
            V.tensor_scalar(neg[:], cnt[:], 0.5, ABSENT, ALU.is_lt, ALU.mult).then_inc(v_neg, 1)
            dve.wait_ge(v_ktm, 1)
            V.tensor_copy(khi[:], ktm[:]).then_inc(v_khi, 1)
            V.tensor_tensor(cb[:], cnt[:].unsqueeze(2).to_broadcast([P, NG, BG]),
                            bm[:].unsqueeze(1).to_broadcast([P, NG, BG]), ALU.mult).then_inc(v_cb, 1)
            dve.wait_ge(v_khi, 1)
            V.tensor_tensor(klo[:], ktm[:], khi[:].bitcast(F32), ALU.subtract).then_inc(v_klo, 1)
            dve.wait_ge(p_q, 1)
            V.tensor_copy(qs[0:64, :], psg[3][0:64, 0:P]).then_inc(v_qhi, 1)
            dve.wait_ge(v_qhi, 1)
            V.tensor_tensor(qs[64:P, :], psg[3][0:64, 0:P], qs[0:64, :].bitcast(F32), ALU.subtract).then_inc(v_qs, 1)
            dve.wait_ge(p_v, 1)
            V.tensor_tensor(vo[:, 0:KVD].rearrange("p (k d) -> p k d", k=KV),
                            psg[2][:, 0:KVD].rearrange("p (k d) -> p k d", k=KV),
                            bm[:].unsqueeze(2).to_broadcast([P, KV, HD]), ALU.mult).then_inc(v_vo, 1)
            V.tensor_copy(vo[:, KVD:VW], bm[:]).then_inc(v_vo, 1)
            dve.wait_ge(p_cnt, 1)
            V.tensor_copy(cpos[:], pswt[1][:, 0:B]).then_inc(v_cpos, 1)
            V.tensor_scalar(cabs[:], pswt[1][:, 0:B], 0.5, ABSENT, ALU.is_lt, ALU.mult).then_inc(v_cpos, 1)
            V.tensor_scalar(sel4[:].rearrange("p (n l) -> p n l", l=L), jdx[0:64, :].unsqueeze(2).to_broadcast([64, GB, L]),
                            pnum[0:64, 0:1], -1.0, ALU.is_equal, ALU.mult).then_inc(c_sel, 1)
            V.tensor_scalar(ident2[:], ridx[:], float(P), 2.0, ALU.is_equal, ALU.mult).then_inc(c_ident, 1)
            V.tensor_scalar(identr[:], ridx[:], float(P), None, ALU.is_equal).then_inc(c_ident, 1)

            def threshold(w):
                dve.wait_ge(p_gam[w], 1)
                V.tensor_scalar(thr[:, w:w + 1], pswt[1][:, 500:501], 0.5 / (D * F), 0.5 * EPS,
                                ALU.mult, ALU.add).then_inc(v_thr, 1)

            def ternary(w, q):
                dve.wait_ge(v_thr, w + 1)
                dve.wait_ge((a_sgn, g_sgn)[w], q // 2 + 1)
                c = slice(512 * q, 512 * q + 512)
                V.scalar_tensor_tensor(tern[:, w, c], aw[:, w, c], thr[:, w:w + 1], sg[:, w, c], ALU.is_gt, ALU.mult).then_inc(v_tern, 1)

            def maxima(g):
                dve.wait_ge(p_s, g + 1)
                if g == 0:
                    dve.wait_ge(c_misc, 2)
                V.tensor_reduce(mx[:, g, :], psg[g][:, :].rearrange("p (n l) -> p n l", l=L), AX_X, ALU.max).then_inc(v_mx, 1)

                dve.wait_ge(v_mx, g + 1)
                V.tensor_copy(mxr[:, g, 0:GB], mx[:, g, :]).then_inc(v_mhi, 1)
                dve.wait_ge(v_mhi, g + 1)
                V.tensor_tensor(mxr[:, g, 32:32 + GB], mx[:, g, :], mxr[:, g, 0:GB].bitcast(F32), ALU.subtract).then_inc(v_mlo, 1)

            def normalise(g):
                dve.wait_ge(p_ctx, g + 1)
                src = psg[g][:, 0:BG * VW].rearrange("p (b v) -> p b v", b=BG)
                V.reciprocal(rec[:, g, :].rearrange("p (b k) -> p b k", b=BG), src[:, :, KVD:VW]).then_inc(v_rec, 1)
                dve.wait_ge(v_rec, g + 1)
                V.tensor_tensor(cn[:, g, :].rearrange("p (b k d) -> p b k d", b=BG, k=KV),
                                src[:, :, 0:KVD].rearrange("p b (k d) -> p b k d", k=KV),
                                rec[:, g, :].rearrange("p (b k) -> p b k", b=BG).unsqueeze(3).to_broadcast([P, BG, KV, HD]),
                                ALU.mult).then_inc(v_cn, 1)

            def table_bias():
                dve.wait_ge(d_bo, 16)
                V.scalar_tensor_tensor(eb[:], emb4[:], EMB_SCALE, bo_bc[:], ALU.mult, ALU.add).then_inc(v_eb, 1)

            def residual_stats(h):
                gs = range(h * HALF, (h + 1) * HALF)
                for g in gs:
                    dve.wait_ge(p_wo, g + 1)
                    if g == 0:
                        dve.wait_ge(v_eb, 1)
                    V.tensor_tensor(hq[:, g, :], psg[g][:, 0:D], eb[:], ALU.add).then_inc(v_hq, 1)
                for g in gs:
                    dve.wait_ge(v_hq, g + 1)
                    V.bn_stats(st2[:, g, :], hq[:, g, :]).then_inc(v_st2, 1)
                for g in gs:
                    dve.wait_ge(v_st2, g + 1)
                    V.bn_aggr(mv2[:, g, :], st2[:, g, :]).then_inc(v_mv2, 1)
                for g in gs:
                    dve.wait_ge(v_mv2, g + 1)
                    V.tensor_scalar(ve2[:, g:g + 1], mv2[:, g, 1:2], EPS, None, ALU.add).then_inc(v_ve2, 1)

            def norm_rows(g):
                dve.wait_ge(g_rs2, g // HALF + 1)
                V.tensor_scalar(xn2[:, g, :], hq[:, g, :], mv2[:, g, 0:1], rs2[:, g:g + 1], ALU.subtract, ALU.mult).then_inc(v_xn2, 1)

            def x_lo(g):
                dve.wait_ge(a_xhi, g + 1)
                V.tensor_tensor(xlo[:, :, g, :], psg[g][:, 0:KC * P].rearrange("p (k n) -> p k n", k=KC),
                                xhi[:, :, g, :].bitcast(F32), ALU.subtract).then_inc(v_xlo, 1)

            def hidden_lo(h, j):
                n = h * FC + j
                dve.wait_ge(a_hr, n + 1)
                dve.wait_ge(a_hh, n + 1)
                V.tensor_tensor(hl[:, n, :], hr[:, n % NHR, :], hh[:, n, :].bitcast(F32), ALU.subtract).then_inc(v_hl, 1)

            def final_lo(g):
                dve.wait_ge(a_fhi, g + 1)
                V.tensor_tensor(flo[:, g, :], psmisc[g % 2][:, 0:D], fhi[:, g, :].bitcast(F32), ALU.subtract).then_inc(v_flo, 1)

            def result(g):
                for b in range(2, BG):
                    dve.wait_ge(p_out, g * BG + b + 1)
                    ins = V.tensor_copy(osb[:, g, b, :], out_banks(g)[b][:, 0:D])
                ins.then_inc(v_out, 1)

            maxima(0)
            maxima(1)
            maxima(2)
            maxima(3)
            threshold(0)
            ternary(0, 0)
            normalise(0)
            normalise(1)
            ternary(0, 1)
            ternary(0, 2)
            table_bias()
            normalise(2)
            ternary(0, 3)
            residual_stats(0)
            normalise(3)
            threshold(1)
            norm_rows(0)
            norm_rows(1)
            ternary(1, 0)
            ternary(1, 1)
            x_lo(0)
            x_lo(1)
            ternary(1, 2)
            ternary(1, 3)
            residual_stats(1)
            norm_rows(2)
            hidden_lo(0, 0)
            hidden_lo(0, 1)
            hidden_lo(0, 2)
            norm_rows(3)
            hidden_lo(0, 3)
            hidden_lo(0, 4)
            hidden_lo(0, 5)
            x_lo(2)
            x_lo(3)
            hidden_lo(0, 6)
            hidden_lo(0, 7)
            final_lo(0)
            final_lo(1)
            hidden_lo(1, 0)
            hidden_lo(1, 1)
            hidden_lo(1, 2)
            result(0)
            result(1)
            hidden_lo(1, 3)
            hidden_lo(1, 4)
            hidden_lo(1, 5)
            hidden_lo(1, 6)
            hidden_lo(1, 7)
            final_lo(2)
            final_lo(3)
            result(2)
            result(3)

        @block.tensor
        def _(pe):
            mm = nc.tensor.matmul
            def warm_up(n):
                for _ in range(n):
                    mm(psg[0][:, :], warm[:, 0:P], warm[:], start=True, stop=True)

            pe.wait_ge(v_warm, 1)
            warm_up(10)
            pe.wait_ge(v_xn1, 1)
            pe.wait_ge(c_ident, 1)
            for k in range(KC):
                ins = nc.tensor.transpose(psmisc[0][:, k * P:(k + 1) * P], xn1[:, k * P:(k + 1) * P], identf[:])
            ins.then_inc(p_xT1, 1)
            pe.wait_ge(v_lev, 1)
            pe.wait_ge(c_sel, 1)
            levels = lev[:].rearrange("b (s e) -> b s e", e=2)[:, :, 1]
            for g in range(NG):
                ins = mm(pswt[0][:, g * S:(g + 1) * S], selb[:, g * P:(g + 1) * P], levels, start=True, stop=True)
            ins.then_inc(p_lev, 1)
            warm_up(1)
            pe.wait_ge(a_xT1, 1)
            pe.wait_ge(a_wk, 1)
            for k in range(KC):
                mm(psmisc[1][:, 0:L], wk[:, k].rearrange("p r n -> p (r n)"), xT1[:, k, 0:L], start=(k == 0), stop=False)
            pe.wait_ge(a_bkr, 1)
            pe.wait_ge(c_ones, 1)
            mm(psmisc[1][:, 0:L], bkr[:].rearrange("p r n -> p (r n)"), ones[0:1, 0:L], start=False, stop=True).then_inc(p_k, 1)
            pe.wait_ge(a_wqh, KC)
            for h in range(G):
                for k in range(KC):
                    mm(psg[3][0:64, h * L:(h + 1) * L], wqh[:, k, h], xT1[:, k, 0:L], start=(h == 0 and k == 0), stop=False,
                       skip_group_check=True)
            pe.wait_ge(a_bqr, 1)
            for h in range(G):
                ins = mm(psg[3][0:64, h * L:(h + 1) * L], bqr[:, h], ones[0:1, 0:L], start=False, stop=True, skip_group_check=True)
            ins.then_inc(p_q, 1)
            pe.wait_ge(d_wv, 16)
            for k in range(KC):
                mm(psg[2][:, 0:KVD], xT1[:, k, :], wv[:, k, :], start=(k == 0), stop=False)
            pe.wait_ge(d_bv, 16)
            mm(psg[2][:, 0:KVD], ones[0:1, :], bvr[:], start=False, stop=True).then_inc(p_v, 1)
            warm_up(1)
            pe.wait_ge(v_cb, 1)
            pe.wait_ge(c_rep, 1)
            mm(pswt[1][:, 0:B], rep[:], cb[:].rearrange("p g b -> p (g b)"), start=True, stop=True).then_inc(p_cnt, 1)

            def scores(g):
                if g == 0:
                    pe.wait_ge(v_qs, 1)
                    pe.wait_ge(v_klo, 1)
                    pe.wait_ge(v_neg, 1)
                    pe.wait_ge(c_ident, 2)
                if g == 2:
                    pe.wait_ge(v_vo, 1)
                mm(psg[g][:, :], qs[:], khi[:].unsqueeze(1).to_broadcast([P, BG, P]), start=True, stop=False)
                mm(psg[g][:, :], qs[:], klo[:].unsqueeze(1).to_broadcast([P, BG, P]), start=False, stop=False)
                mm(psg[g][:, :], neg[:, g:g + 1].to_broadcast([P, P]),
                   identb[:].rearrange("p (b l) -> p b l", b=BG).unsqueeze(2).to_broadcast([P, BG, KV, L]),
                   start=False, stop=True).then_inc(p_s, 1)

            def max_t(g):
                pe.wait_ge(v_mlo, g + 1)
                if g >= 2:
                    pe.wait_ge(a_ms, g - 1)
                nc.tensor.transpose(psmisc[g % 2][0:64, 0:P], mxr[:, g, :].bitcast(F32),
                                    identf[:]).then_inc(p_mt, 1)

            def exponents(g):
                rhs = qs[:].unsqueeze(1).to_broadcast([P, BG, P])
                mm(psg[g][:, :], khi[:], rhs, start=True, stop=False)
                mm(psg[g][:, :], klo[:], rhs, start=False, stop=True)
                pe.wait_ge(a_ms, g + 1)
                pe.wait_ge(c_sel, 2)
                for b in range(BG):
                    ins = mm(psg[g][:, b * P:(b + 1) * P], sel4[:, b * P:(b + 1) * P], ms[:, g, :], start=False, stop=True,
                             skip_group_check=True)
                ins.then_inc(p_et, 1)

            def context(g):
                pe.wait_ge(g_voc, g + 1)
                pe.wait_ge(a_exp, BG * (g + 1))
                for b in range(BG):
                    ins = mm(psg[g][:, b * VW:(b + 1) * VW], et[:, g, b, :], voc[:, g * BG + b, :], start=True, stop=True)
                ins.then_inc(p_ctx, 1)

            def context_t(g):
                pe.wait_ge(v_cn, g + 1)
                for b in range(BG):
                    ins = nc.tensor.transpose(psg[g][0:64, b * P:(b + 1) * P], cn[:, g, b * KVD:(b + 1) * KVD], identf[:])
                ins.then_inc(p_cT, 1)

            def out_proj(g):
                pe.wait_ge(a_cT, 2 * (g + 1))
                if g == 0:
                    for i in range(4):
                        pe.wait_ge(d_wo[i], 16)
                for e in range(H2):
                    ins = mm(psg[g][:, 0:D], cT[:, g, e].rearrange("p b l -> p (b l)"), wo[:, e, :], start=(e == 0), stop=(e == H2 - 1))
                ins.then_inc(p_wo, 1)

            def rows_t(g):
                pe.wait_ge(v_xn2, g + 1)
                for k in range(KC):
                    ins = nc.tensor.transpose(psg[g][:, k * P:(k + 1) * P], xn2[:, g, k * P:(k + 1) * P], identf[:])
                ins.then_inc(p_xT2, 1)

            def abs_total(w):
                pe.wait_ge(a_abs, 2 * (w + 1))
                if w == 0:
                    pe.wait_ge(v_cpos, 2)
                else:
                    pe.wait_ge(v_thr, 1)
                for i in range(2):
                    ins = mm(pswt[1][:, 500:501], ones[:], asum[:, 2 * w + i:2 * w + i + 1], start=(i == 0), stop=(i == 1))
                ins.then_inc(p_gam[w], 1)

            def weights_t(u):
                w, i = divmod(u, 4)
                if w == 0:
                    pe.wait_ge(v_tern, i + 1)
                    if u == 1:
                        pe.wait_ge(v_thr, 2)
                    elif u >= 2:
                        pe.wait_ge(a_wt, u - 1)
                elif i < 2:
                    pe.wait_ge(v_tern, 8)
                    pe.wait_ge(v_xlo, i + 1)
                    pe.wait_ge(c_ident, 3)
                else:
                    pe.wait_ge(a_wt, u - 1)
                for jj in range(2):
                    for k in range(KC):
                        j = 2 * i + jj
                        if w == 0:
                            src = tern[:, 0, j * D + k * P:j * D + (k + 1) * P]
                        else:
                            src = tern[:, 1, k * F:(k + 1) * F].rearrange("p (f j) -> p j f", j=FC)[:, j]
                        ins = mm((pswt, psg)[w][u % 2][:, (jj * KC + k) * P:(jj * KC + k + 1) * P], src, (identb, ident2)[w][:],
                                 start=True, stop=True)
                ins.then_inc(p_wt, 1)

            def ffn1(h, j):
                n = h * FC + j
                if n < 2:
                    pe.wait_ge(a_wt, 3 + n)
                elif n == 2:
                    pe.wait_ge(a_wt, 4)
                if j == 0:
                    pe.wait_ge(v_xlo, HALF * (h + 1))
                if n >= 2:
                    pe.wait_ge(a_hh, n - 1)
                for m, part in enumerate((xhi, xlo)):
                    for k in range(KC):
                        ins = mm(pswt[n % 2][:, 0:RH], w1T[:, j, k, :], part[:, k, HALF * h:HALF * (h + 1), :].rearrange("p g n -> p (g n)"),
                                 start=(m == 0 and k == 0), stop=(m == 1 and k == KC - 1))
                ins.then_inc(p_f1, 1)

            def residual(g):
                pe.wait_ge(g_hbl, g + 1)
                if g == 0:
                    pe.wait_ge(c_ident, 4)
                if g == 0:
                    pe.wait_ge(a_ms, 4)
                if g >= HALF:
                    pe.wait_ge(v_flo, g - HALF + 1)
                mm(psmisc[g % HALF][:, 0:D], identr[:], hbh[:, g, :], start=True, stop=False)
                mm(psmisc[g % HALF][:, 0:D], identr[:], hbl[:, g, :], start=False, stop=False)

            def ffn2(j, g):
                n = g // HALF * FC + j
                r = g % HALF
                pe.wait_ge(v_hl, n + 1)
                if g < HALF and j % 2 == 0:
                    pe.wait_ge(a_wt, 5 + j // 2)
                for m, part in enumerate((hh, hl)):
                    ins = mm(psmisc[r][:, 0:D], part[:, n, r * P:(r + 1) * P], w2T[:, j, :],
                             start=False, stop=(j == FC - 1 and m == 1))
                if j == FC - 1:
                    ins.then_inc(p_acc, 1)

            def spread(g):
                pe.wait_ge(v_flo, g + 1)
                if g == 0:
                    pe.wait_ge(a_wt, 8)
                    pe.wait_ge(v_xlo, NG)
                for b in range(BG):
                    if g == NG - 1 and b < 2:
                        pe.wait_ge(a_hh, NH)
                    elif g == NG - 1 and b == 2:
                        pe.wait_ge(v_flo, 3)
                    elif g == NG - 1:
                        pe.wait_ge(a_out, g)
                    elif g >= 1:
                        pe.wait_ge((a_out, v_out)[b // 2], g)
                    q = slice(L * b, L * (b + 1))
                    mm(out_banks(g)[b][:, 0:D], oh[q, g, :], fhi[q, g, :], start=True, stop=False)
                    mm(out_banks(g)[b][:, 0:D], oh[q, g, :], flo[q, g, :], start=False, stop=True).then_inc(p_out, 1)

            scores(0)
            scores(1)
            scores(2)
            scores(3)
            max_t(0)
            abs_total(0)
            max_t(1)
            exponents(0)
            max_t(2)
            exponents(1)
            exponents(2)
            max_t(3)
            context(0)
            context(1)
            exponents(3)
            context_t(0)
            context_t(1)
            context(2)
            out_proj(0)
            out_proj(1)
            weights_t(0)
            context(3)
            abs_total(1)
            context_t(2)
            context_t(3)
            weights_t(1)
            rows_t(0)
            weights_t(2)
            rows_t(1)
            out_proj(2)
            weights_t(3)
            out_proj(3)
            ffn1(0, 0)
            ffn1(0, 1)
            residual(0)
            weights_t(4)
            weights_t(5)
            ffn1(0, 2)
            residual(1)
            ffn1(0, 3)
            weights_t(6)
            weights_t(7)
            rows_t(2)
            ffn1(0, 4)
            ffn2(0, 1)
            ffn1(0, 5)
            ffn2(1, 1)
            ffn2(0, 0)
            ffn2(1, 0)
            ffn2(2, 1)
            rows_t(3)
            ffn1(0, 6)
            ffn1(0, 7)
            ffn2(3, 1)
            ffn2(4, 1)
            ffn2(5, 1)
            ffn2(2, 0)
            ffn2(3, 0)
            ffn1(1, 0)
            ffn2(4, 0)
            ffn2(5, 0)
            ffn2(6, 0)
            ffn2(7, 0)
            ffn1(1, 1)
            ffn2(6, 1)
            ffn2(7, 1)
            ffn1(1, 2)
            residual(2)
            ffn1(1, 3)
            spread(0)
            ffn1(1, 4)
            ffn1(1, 5)
            ffn2(0, 2)
            spread(1)
            ffn1(1, 6)
            ffn2(1, 2)
            ffn1(1, 7)
            ffn2(2, 2)
            ffn2(3, 2)
            residual(3)
            ffn2(4, 2)
            ffn2(0, 3)
            ffn2(5, 2)
            ffn2(1, 3)
            ffn2(2, 3)
            ffn2(6, 2)
            ffn2(7, 2)
            ffn2(3, 3)
            ffn2(4, 3)
            ffn2(5, 3)
            ffn2(6, 3)
            ffn2(7, 3)
            spread(2)
            spread(3)


_INS = ["x", "L0_tok_level_emb", "L0_attn_Wq", "L0_attn_bq", "L0_attn_Wk", "L0_attn_bk", "L0_attn_Wv", "L0_attn_bv",
        "L0_attn_Wo", "L0_attn_bo", "L0_ffn_W1", "L0_ffn_b1", "L0_ffn_W2", "L0_ffn_b2"]


def kernel(**inputs):
    import numpy as _np
    import concourse.bacc as _bacc
    from concourse import mybir as _mybir
    from concourse.bass_utils import run_bass_kernel_spmd as _run

    nc = _bacc.Bacc("TRN2", target_bir_lowering=False, num_devices=1)
    arrays, args = {}, []
    for name in _INS:
        a = _np.ascontiguousarray(inputs[name])
        arrays[f"in_{name}_dram"] = a
        args.append(nc.dram_tensor(f"in_{name}_dram", a.shape, _mybir.dt.from_np(a.dtype), kind="ExternalInput").ap())
    shape = tuple(inputs["x"].shape) + (inputs["L0_tok_level_emb"].shape[1],)
    args.append(nc.dram_tensor("out_0_dram", shape, _mybir.dt.float32, kind="ExternalOutput").ap())
    level_tower(nc, *args)
    r = _run(nc, [arrays], core_ids=[0])
    return r.results[0]["out_0_dram"]
```

```python
from contextlib import ExitStack

import concourse.bass as bass
from concourse import mybir

F32 = mybir.dt.float32
F32R = mybir.dt.float32r
BF16 = mybir.dt.bfloat16
I32 = mybir.dt.int32
ALU = mybir.AluOpType
ACT = mybir.ActivationFunctionType
AX_X = mybir.AxisListType.X

P = 128
OPEN_TOKENS = (40, 91, 123)
CLOSE_TOKENS = (41, 93, 125)
EMB_SCALE = 0.15
EPS = 1e-5
ABSENT = -1e30


def level_tower(nc, x, emb, Wq, bq, Wk, bk, Wv, bv, Wo, bo, W1, b1, W2, b2, out):
    B, S = x.shape
    L, D = emb.shape
    KVD = Wk.shape[1]
    HD = 16
    KV = KVD // HD
    G = D // HD // KV
    F = W1.shape[0]
    KC = D // P
    FC = F // P
    BG = P // L
    NG = B // BG
    HALF = NG // 2
    H2 = G // 2
    GB = BG * KV
    RH = HALF * P
    VW = KVD + KV
    SCALE = float(HD) ** -0.5
    assert S == P and L == 32 and D == 2 * P and G == 4 and KV == 4 and NG == 4 and F % P == 0

    ctx = ExitStack()
    with ctx:
        def sb(name, shape, dt=F32):
            return ctx.enter_context(nc.sbuf_tensor(name, shape, dt))

        def sem(name):
            return ctx.enter_context(nc.semaphore(name))

        pswt = [ctx.enter_context(nc.psum_tensor(f"pswt{i}", [P, 512], F32)) for i in range(2)]
        psmisc = [ctx.enter_context(nc.psum_tensor(f"psmisc{i}", [P, 512], F32)) for i in range(2)]
        psg = [ctx.enter_context(nc.psum_tensor(f"psg{i}", [P, 512], F32)) for i in range(NG)]

        tok = sb("tok", [B, S], I32)
        emb1 = sb("emb1", [L, D])
        emb4 = sb("emb4", [P, D])
        wq = sb("wq", [P, KC, D])
        wqh = sb("wqh", [P, KC, G, KVD])
        wk1 = sb("wk1", [P, KC, KVD])
        bk1 = sb("bk1", [1, KVD])
        wk = sb("wk", [P, KC, 2, KVD])
        wv = sb("wv", [P, KC, KVD])
        brow = sb("brow", [1, D])
        bqr = sb("bqr", [1, G, KVD])
        bkr = sb("bkr", [1, 2, KVD])
        bvr = sb("bvr", [1, KVD])
        wo = sb("wo", [P, H2, D])
        bo_bc = sb("bo_bc", [P, D])
        b2_bc = sb("b2_bc", [P, D])
        b1c = sb("b1c", [P, FC])
        w1 = sb("w1", [P, FC, D])
        w2 = sb("w2", [P, KC, F])
        identf = sb("identf", [P, P])
        ident2 = sb("ident2", [P, P], BF16)
        identr = sb("identr", [P, P], F32R)
        identb = sb("identb", [P, P], BF16)
        ones = sb("ones", [P, P])
        sel4 = sb("sel4", [64, 512], F32R)
        selb = sb("selb", [B, 512], BF16)
        bm = sb("bm", [P, BG])
        km = sb("km", [P, KV])
        pidx = sb("pidx", [P, 1], I32)
        pint = sb("pint", [P, 3], I32)
        pnum = sb("pnum", [P, 3])
        ridx = sb("ridx", [P, P], I32)
        rmod = sb("rmod", [P, P], I32)
        jdx = sb("jdx", [P, GB], I32)
        warm = sb("warm", [P, 512], BF16)
        tiny = sb("tiny", [1, 2])
        rep = sb("rep", [P, P], BF16)
        mhalf = sb("mhalf", [P, 1])
        cmp = sb("cmp", [B, 7, S])
        sc0 = sb("sc0", [B, 2 * S])
        sc1 = sb("sc1", [B, 2 * S])
        lev = sb("lev", [B, 2 * S], BF16)
        oh = sb("oh", [P, NG, S], F32R)
        cnt = sb("cnt", [P, NG])
        neg = sb("neg", [P, NG], BF16)
        cb = sb("cb", [P, NG, BG], BF16)
        cpos = sb("cpos", [P, B])
        cabs = sb("cabs", [P, B])
        st1 = sb("st1", [L, 6])
        mv1 = sb("mv1", [L, 2])
        ve1 = sb("ve1", [L, 1])
        rs1 = sb("rs1", [L, 1])
        xn1 = sb("xn1", [L, D])
        xT1 = sb("xT1", [P, KC, P])
        qs = sb("qs", [P, P], F32R)
        ktm = sb("ktm", [P, P])
        khi = sb("khi", [P, P], F32R)
        klo = sb("klo", [P, P], F32R)
        vo = sb("vo", [P, VW])
        voc = sb("voc", [P, B, VW])
        eb = sb("eb", [P, D])
        mx = sb("mx", [P, NG, GB])
        mxr = sb("mxr", [P, NG, 64], F32R)
        ms = sb("ms", [64, NG, P], F32R)
        et = sb("et", [P, NG, BG, P])
        rec = sb("rec", [P, NG, GB])
        cn = sb("cn", [P, NG, BG * KVD])
        cT = sb("cT", [P, NG, H2, BG, L])
        hq = sb("hq", [P, NG, D])
        hb = sb("hb", [P, NG, D])
        hbh = sb("hbh", [P, NG, D], F32R)
        hbl = sb("hbl", [P, NG, D], F32R)
        st2 = sb("st2", [P, NG, 6])
        mv2 = sb("mv2", [P, NG, 2])
        ve2 = sb("ve2", [P, NG])
        rs2 = sb("rs2", [P, NG])
        xn2 = sb("xn2", [P, NG, D])
        xhi = sb("xhi", [P, KC, NG, P], F32R)
        xlo = sb("xlo", [P, KC, NG, P], F32R)
        asum = sb("asum", [P, 4])
        gam = sb("gam", [P, 4])
        thr = sb("thr", [P, 2])
        aw = sb("aw", [P, 2, 2048])
        sg = sb("sg", [P, 2, 2048], BF16)
        tern = sb("tern", [P, 2, 2048], BF16)
        w1T = sb("w1T", [P, FC, KC, P], F32R)
        w2T = sb("w2T", [P, FC, D], F32R)
        NHR = 4
        NH = 2 * FC
        hr = sb("hr", [P, NHR, RH])
        hh = sb("hh", [P, NH, RH], F32R)
        hl = sb("hl", [P, NH, RH], F32R)
        fin = sb("fin", [P, HALF, D])
        fhi = sb("fhi", [P, NG, D], F32R)
        flo = sb("flo", [P, NG, D], F32R)
        osb = aw[:].rearrange("p w n -> p (w n)").rearrange("p (g b d) -> p g b d", g=NG, b=BG)

        d_tok, d_emb, d_emb4, d_wq, d_wk, d_wv, d_bq, d_bk, d_bv = (sem("d_" + n) for n in "tok emb emb4 wq wk wv bq bk bv".split())
        d_bo, d_b1, d_b2 = (sem("d_" + n) for n in "bo b1 b2".split())
        d_w1 = [sem(f"d_w1_{i}") for i in range(2)]
        d_w2 = [sem(f"d_w2_{i}") for i in range(2)]
        d_wo = [sem(f"d_wo_{i}") for i in range(4)]
        d_out = sem("d_out")

        c_ones = sem("c_ones")
        c_iota = sem("c_iota")
        c_misc = sem("c_misc")
        c_pnum = sem("c_pnum")
        c_ident = sem("c_ident")
        c_sel = sem("c_sel")
        c_bm = sem("c_bm")
        c_mod = sem("c_mod")
        c_rep = sem("c_rep")
        c_scan = sem("c_scan")
        v_warm = sem("v_warm")
        a_table = sem("a_table")
        v_cmp = sem("v_cmp")
        v_pair = sem("v_pair")
        v_sum = sem("v_sum")
        v_lev = sem("v_lev")
        p_lev = sem("p_lev")
        v_oh = sem("v_oh")
        v_cnt = sem("v_cnt")
        v_neg = sem("v_neg")
        v_cb = sem("v_cb")
        p_cnt = sem("p_cnt")
        v_cpos = sem("v_cpos")
        v_st1 = sem("v_st1")
        v_mv1 = sem("v_mv1")
        v_ve1 = sem("v_ve1")
        g_rs1 = sem("g_rs1")
        v_xn1 = sem("v_xn1")
        p_xT1 = sem("p_xT1")
        a_xT1 = sem("a_xT1")
        p_k = sem("p_k")
        p_q = sem("p_q")
        p_v = sem("p_v")
        v_ktm = sem("v_ktm")
        v_khi = sem("v_khi")
        v_klo = sem("v_klo")
        v_qhi = sem("v_qhi")
        v_qs = sem("v_qs")
        v_vo = sem("v_vo")
        v_eb = sem("v_eb")
        g_voc = sem("g_voc")
        a_bqr = sem("a_bqr")
        a_wk = sem("a_wk")
        a_bkr = sem("a_bkr")
        a_wqh = sem("a_wqh")
        p_s = sem("p_s")
        v_mx = sem("v_mx")
        p_mt = sem("p_mt")
        a_ms = sem("a_ms")
        v_mhi = sem("v_mhi")
        v_mlo = sem("v_mlo")
        p_et = sem("p_et")
        a_exp = sem("a_exp")
        p_ctx = sem("p_ctx")
        v_rec = sem("v_rec")
        v_cn = sem("v_cn")
        p_cT = sem("p_cT")
        a_cT = sem("a_cT")
        p_wo = sem("p_wo")
        v_hq = sem("v_hq")
        g_hb = sem("g_hb")
        g_hbh = sem("g_hbh")
        g_hbl = sem("g_hbl")
        v_st2 = sem("v_st2")
        v_mv2 = sem("v_mv2")
        v_ve2 = sem("v_ve2")
        g_rs2 = sem("g_rs2")
        v_xn2 = sem("v_xn2")
        p_xT2 = sem("p_xT2")
        a_xhi = sem("a_xhi")
        v_xlo = sem("v_xlo")
        a_abs = sem("a_abs")
        a_sgn = sem("a_sgn")
        g_sgn = sem("g_sgn")
        p_gam = [sem(f"p_gam{i}") for i in range(2)]
        v_part = sem("v_part")
        v_thr = sem("v_thr")
        v_tern = sem("v_tern")
        p_wt = sem("p_wt")
        a_wt = sem("a_wt")
        p_f1 = sem("p_f1")
        a_hr = sem("a_hr")
        a_hh = sem("a_hh")
        v_hh = sem("v_hh")
        v_hl = sem("v_hl")
        p_acc = sem("p_acc")
        a_fhi = sem("a_fhi")
        v_sumf = sem("v_sumf")
        v_flo = sem("v_flo")
        p_out = sem("p_out")
        a_out = sem("a_out")
        v_out = sem("v_out")


        ROUND_ON_VECTOR = (0, 1, 2, 5, 6, 8, 11, 12, 14)

        def rounded_by_act(n):
            return sum(m not in ROUND_ON_VECTOR for m in range(n + 1))

        def rounded_by_dve(n):
            return sum(m in ROUND_ON_VECTOR for m in range(n + 1))

        block = ctx.enter_context(nc.Block())

        w1_rows = W1.rearrange("(p j) d -> p j d", j=FC)
        w2_rows = W2.rearrange("(c p) f -> p c f", p=P)
        wo_rows = Wo.rearrange("(k a e d) n -> a e k d n", k=KV, a=2, e=H2)

        def halves(w, i):
            return w1[:, i * FC // 2:(i + 1) * FC // 2, :].rearrange("p j d -> p (j d)") if w == 0 else w2[:, i, :]

        def out_banks(g):
            return psg if g < NG - 1 else [pswt[0], pswt[1], psmisc[0], psg[0]]

        @block.sync
        def _(sp):
            sp.dma_start(emb1[:], emb).then_inc(d_emb, 16)
            sp.dma_start(wk1[:], Wk.rearrange("(c p) n -> p c n", p=P)).then_inc(d_wk, 16)
            sp.dma_start(wq[:], Wq.rearrange("(c p) n -> p c n", p=P)).then_inc(d_wq, 16)
            sp.dma_start(bk1[:], bk.unsqueeze(0)).then_inc(d_bk, 16)
            sp.dma_start(brow[:], bq.unsqueeze(0)).then_inc(d_bq, 16)
            sp.dma_start(wv[:], Wv.rearrange("(c p) n -> p c n", p=P)).then_inc(d_wv, 16)
            sp.dma_start(bvr[:], bv.unsqueeze(0)).then_inc(d_bv, 16)
            for i in range(2):
                c = slice(i * FC // 2, (i + 1) * FC // 2)
                sp.dma_start(w1[:, c, :], w1_rows[:, c, :]).then_inc(d_w1[i], 16)
            for i in range(2):
                sp.dma_start(w2[:, i, :], w2_rows[:, i, :]).then_inc(d_w2[i], 16)
            for a in range(2):
                for e in range(H2):
                    sp.dma_start(wo[64 * a:64 * a + 64, e, :], wo_rows[a, e]).then_inc(d_wo[2 * a + e], 16)
            sp.dma_start(emb4[:], emb.unsqueeze(0).to_broadcast([BG, L, D])).then_inc(d_emb4, 16)
            sp.dma_start(bo_bc[:], bo.unsqueeze(0).to_broadcast([P, D])).then_inc(d_bo, 16)
            sp.dma_start(b1c[:], b1.rearrange("(p j) -> p j", j=FC)).then_inc(d_b1, 16)
            sp.dma_start(b2_bc[:], b2.unsqueeze(0).to_broadcast([P, D])).then_inc(d_b2, 16)
            out_t = out.rearrange("b s d -> s b d")
            for g in range(NG):
                for e in range(2):
                    if e == 0:
                        sp.wait_ge(a_out, g + 1)
                    else:
                        sp.wait_ge(v_out, g + 1)
                    b0 = g * BG + 2 * e
                    sp.dma_start(out_t[:, b0:b0 + 2, :], osb[:, g, 2 * e:2 * e + 2, :]).then_inc(d_out, 16)
            sp.wait_ge(d_out, 16 * 2 * NG)

        @block.gpsimd
        def _(pool):
            nc.gpsimd.memset(sc0[:], 0.0).then_inc(c_scan, 1)
            nc.gpsimd.memset(sc1[:], 0.0).then_inc(c_scan, 1)
            pool.wait_ge(c_scan, 2)
            nc.gpsimd.memset(sc1[:].rearrange("b (s e) -> b s e", e=2)[:, :, 0:1], float(1 - L)).then_inc(c_scan, 1)
            nc.gpsimd.iota(pidx[:], pattern=[[0, 1]], base=0, channel_multiplier=1).then_inc(c_iota, 1)
            nc.gpsimd.iota(ridx[:], pattern=[[-1, P]], base=P, channel_multiplier=1).then_inc(c_iota, 1)
            nc.gpsimd.iota(jdx[:], pattern=[[1, GB]], base=0, channel_multiplier=0).then_inc(c_iota, 1)
            nc.gpsimd.memset(mhalf[:], -0.5).then_inc(c_misc, 1)
            nc.gpsimd.memset(ones[:], 1.0).then_inc(c_ones, 1)
            pool.wait_ge(v_ve1, 1)
            pool.wait_ge(c_misc, 1)
            nc.gpsimd.tensor_tensor(rs1[:], ve1[:], mhalf[0:L, :], ALU.pow).then_inc(g_rs1, 1)
            nc.gpsimd.memset(mxr[:].bitcast(F32), 0.0).then_inc(c_misc, 1)
            pool.wait_ge(v_vo, 2)
            pool.wait_ge(v_cpos, 2)
            for g in range(NG):
                bs = slice(g * BG, (g + 1) * BG)
                nc.gpsimd.tensor_tensor(voc[:, bs, :], vo[:].unsqueeze(1).to_broadcast([P, BG, VW]),
                                        cpos[:, bs].unsqueeze(2).to_broadcast([P, BG, VW]), ALU.mult).then_inc(g_voc, 1)
            for i in range(2):
                pool.wait_ge(d_w2[i], 16)
                nc.gpsimd.tensor_scalar(sg[:, 1, i * 1024:(i + 1) * 1024], halves(1, i), 0.0, 0.5,
                                        ALU.is_ge, ALU.subtract).then_inc(g_sgn, 1)
            pool.wait_ge(d_b2, 16)
            for h in range(NG // HALF):
                gs = range(h * HALF, (h + 1) * HALF)
                c = slice(h * HALF, (h + 1) * HALF)
                pool.wait_ge(v_ve2, (h + 1) * HALF)
                nc.gpsimd.tensor_tensor(rs2[:, c], ve2[:, c], mhalf[:].to_broadcast([P, HALF]), ALU.pow).then_inc(g_rs2, 1)
                for g in gs:
                    nc.gpsimd.tensor_tensor(hb[:, g, :], hq[:, g, :], b2_bc[:], ALU.add).then_inc(g_hb, 1)
                if h == 0:
                    continue
                for g in gs:
                    pool.wait_ge(g_hb, g + 1)
                    nc.gpsimd.tensor_copy(hbh[:, g, :], hb[:, g, :]).then_inc(g_hbh, 1)
                for g in gs:
                    pool.wait_ge(g_hbh, g - HALF + 1)
                    nc.gpsimd.tensor_tensor(hbl[:, g, :], hb[:, g, :], hbh[:, g, :].bitcast(F32), ALU.subtract).then_inc(g_hbl, 1)

        @block.scalar
        def _(act):
            act.dma_start(tok[:], x).then_inc(d_tok, 16)
            act.wait_ge(v_warm, 2)
            nc.scalar.activation(tiny[0:1, 1:2], tiny[0:1, 0:1], ACT.Exp).then_inc(a_table, 1)
            act.wait_ge(d_wk, 16)
            nc.scalar.activation(wk[:], wk1[:].unsqueeze(2).to_broadcast([P, KC, 2, KVD]), ACT.Copy).then_inc(a_wk, 1)
            act.wait_ge(d_wq, 16)
            for k in range(KC):
                nc.scalar.activation(wqh[:, k].rearrange("p h (k d) -> p h k d", k=KV),
                                     wq[:, k, :].rearrange("p (k h d) -> p h k d", k=KV, h=G), ACT.Copy).then_inc(a_wqh, 1)
            act.wait_ge(d_bk, 16)
            nc.scalar.activation(bkr[:], bk1[:].unsqueeze(1).to_broadcast([1, 2, KVD]), ACT.Copy).then_inc(a_bkr, 1)
            act.wait_ge(p_xT1, 1)
            nc.scalar.activation(xT1[:].rearrange("p k (b l) -> p k b l", b=BG),
                                 psmisc[0][:, 0:KC * L].rearrange("p (k l) -> p k l", k=KC).unsqueeze(2).to_broadcast([P, KC, BG, L]),
                                 ACT.Copy).then_inc(a_xT1, 1)
            act.wait_ge(d_bq, 16)
            nc.scalar.activation(bqr[:].rearrange("p h (k d) -> p h k d", k=KV), brow[:].rearrange("p (k h d) -> p h k d", k=KV, h=G),
                                 ACT.Copy).then_inc(a_bqr, 1)

            def magnitudes(w, i):
                act.wait_ge((d_w1, d_w2)[w][i], 16)
                nc.scalar.activation(aw[:, w, i * 1024:(i + 1) * 1024], halves(w, i), ACT.Abs,
                                     accum_out=asum[:, 2 * w + i:2 * w + i + 1]).then_inc(a_abs, 1)

            def signs(i):
                nc.scalar.activation(sg[:, 0, i * 1024:(i + 1) * 1024], halves(0, i), ACT.Sign).then_inc(a_sgn, 1)

            def weights_out(u):
                act.wait_ge(p_wt, u + 1)
                src = (pswt, psg)[u // 4][u % 2][:, :]
                j = 2 * (u % 4)
                if u < 4:
                    nc.scalar.activation(w1T[:, j:j + 2, :, :].rearrange("p j k f -> p (j k f)"), src, ACT.Copy).then_inc(a_wt, 1)
                else:
                    nc.scalar.activation(w2T[:, j:j + 2, :].rearrange("p j d -> p (j d)"), src, ACT.Copy).then_inc(a_wt, 1)

            def max_out(g):
                act.wait_ge(p_mt, g + 1)
                nc.scalar.activation(ms[:, g, :], psmisc[g % 2][0:64, 0:P], ACT.Copy).then_inc(a_ms, 1)

            def exps(g, b):
                act.wait_ge(p_et, g + 1)
                if g == 0 and b == 0:
                    act.wait_ge(v_cpos, 2)
                n = g * BG + b
                nc.scalar.activation(et[:, g, b, :], psg[g][:, b * P:(b + 1) * P], ACT.Exp,
                                     bias=cabs[:, n:n + 1]).then_inc(a_exp, 1)

            def ctx_out(g):
                act.wait_ge(p_cT, g + 1)
                for c in range(2):
                    src = psg[g][64 * c:64 * c + 64, 0:D].rearrange("p (b a e l) -> p a e b l", b=2, a=2, e=H2)
                    for a in range(2):
                        dst = cT[64 * a:64 * a + 64, g].rearrange("p e (b c) l -> p c e b l", c=2)
                        nc.scalar.activation(dst[:, c], src[:, a], ACT.Copy).then_inc(a_cT, 1)

            def x_hi(g):
                act.wait_ge(p_xT2, g + 1)
                nc.scalar.activation(xhi[:, :, g, :], psg[g][:, 0:KC * P].rearrange("p (k n) -> p k n", k=KC),
                                     ACT.Copy).then_inc(a_xhi, 1)

            def hidden(h, j):
                n = h * FC + j
                act.wait_ge(p_f1, n + 1)
                if n == 0:
                    act.wait_ge(d_b1, 16)
                if n >= NHR:
                    act.wait_ge(v_hl, n - NHR + 1)
                nc.scalar.activation(hr[:, n % NHR, :], pswt[n % 2][:, 0:RH], ACT.Relu, bias=b1c[:, j:j + 1]).then_inc(a_hr, 1)
                if n not in ROUND_ON_VECTOR:
                    nc.scalar.activation(hh[:, n, :], pswt[n % 2][:, 0:RH], ACT.Relu, bias=b1c[:, j:j + 1]).then_inc(a_hh, 1)

            def final_hi(g):
                act.wait_ge(p_acc, g + 1)
                nc.scalar.activation(fhi[:, g, :], psmisc[g % 2][:, 0:D], ACT.Copy).then_inc(a_fhi, 1)

            def result(g):
                for b in range(2):
                    act.wait_ge(p_out, g * BG + b + 1)
                    ins = nc.scalar.activation(osb[:, g, b, :], out_banks(g)[b][:, 0:D], ACT.Copy)
                ins.then_inc(a_out, 1)

            magnitudes(0, 0)
            magnitudes(0, 1)
            signs(0)
            magnitudes(1, 0)
            max_out(0)
            signs(1)
            max_out(1)
            max_out(2)
            exps(0, 0)
            exps(0, 1)
            exps(0, 2)
            exps(0, 3)
            exps(1, 0)
            exps(1, 1)
            exps(1, 2)
            exps(1, 3)
            exps(2, 0)
            exps(2, 1)
            max_out(3)
            exps(2, 2)
            exps(2, 3)
            ctx_out(0)
            exps(3, 0)
            exps(3, 1)
            ctx_out(1)
            exps(3, 2)
            exps(3, 3)
            magnitudes(1, 1)
            weights_out(0)
            ctx_out(2)
            weights_out(1)
            ctx_out(3)
            x_hi(0)
            x_hi(1)
            weights_out(2)
            weights_out(3)
            hidden(0, 0)
            hidden(0, 1)
            weights_out(4)
            weights_out(5)
            hidden(0, 2)
            hidden(0, 3)
            hidden(0, 4)
            hidden(0, 5)
            x_hi(2)
            x_hi(3)
            weights_out(6)
            hidden(0, 6)
            hidden(0, 7)
            weights_out(7)
            hidden(1, 0)
            hidden(1, 1)
            hidden(1, 2)
            hidden(1, 3)
            result(0)
            hidden(1, 4)
            hidden(1, 5)
            result(1)
            hidden(1, 6)
            hidden(1, 7)
            final_hi(2)
            final_hi(3)
            result(2)
            result(3)

        @block.vector
        def _(dve):
            V = nc.vector
            V.memset(warm[:], 0.0).then_inc(v_warm, 1)
            V.memset(tiny[:], 0.0).then_inc(v_warm, 1)
            dve.wait_ge(c_iota, 1)
            V.tensor_scalar(pint[:, 0:1], pidx[:], L - 1, None, ALU.bitwise_and).then_inc(c_mod, 1)
            V.tensor_scalar(pint[:, 1:2], pidx[:], 4, KV - 1, ALU.logical_shift_right, ALU.bitwise_and).then_inc(c_mod, 1)
            V.tensor_scalar(pint[:, 2:3], pidx[:], 5, None, ALU.logical_shift_right).then_inc(c_mod, 1)
            dve.wait_ge(c_iota, 2)
            V.tensor_scalar(identf[:], ridx[:], float(P), None, ALU.is_equal).then_inc(c_ident, 1)
            dve.wait_ge(c_mod, 3)
            V.tensor_copy(pnum[:], pint[:]).then_inc(c_pnum, 1)
            dve.wait_ge(c_pnum, 1)
            dve.wait_ge(c_iota, 3)
            V.tensor_scalar(selb[:].rearrange("p (n l) -> p n l", l=L), jdx[0:B, :].unsqueeze(2).to_broadcast([B, GB, L]),
                            pnum[0:B, 0:1], None, ALU.is_equal).then_inc(c_sel, 1)
            dve.wait_ge(d_emb, 16)
            V.bn_stats(st1[:], emb1[:]).then_inc(v_st1, 1)
            dve.wait_ge(d_tok, 16)
            for i, t in enumerate(OPEN_TOKENS):
                V.tensor_scalar(cmp[:, i, :], tok[:], float(t), None, ALU.is_equal).then_inc(v_cmp, 1)
            dve.wait_ge(v_st1, 1)
            V.bn_aggr(mv1[:], st1[:]).then_inc(v_mv1, 1)

            def closing(i, t):
                dve.wait_ge(v_cmp, i + 1)
                V.scalar_tensor_tensor(cmp[:, 3 + i, :], tok[:], float(t), cmp[:, i, :], ALU.is_equal, ALU.subtract).then_inc(v_pair, 1)

            closing(0, CLOSE_TOKENS[0])
            dve.wait_ge(v_mv1, 1)
            V.tensor_scalar(ve1[:], mv1[:, 1:2], EPS / EMB_SCALE ** 2, None, ALU.add).then_inc(v_ve1, 1)
            closing(1, CLOSE_TOKENS[1])
            closing(2, CLOSE_TOKENS[2])
            dve.wait_ge(v_pair, 2)
            V.tensor_tensor(cmp[:, 6, :], cmp[:, 3, :], cmp[:, 4, :], ALU.add).then_inc(v_sum, 1)
            dve.wait_ge(g_rs1, 1)
            V.tensor_scalar(xn1[:], emb1[:], mv1[:, 0:1], rs1[:, 0:1], ALU.subtract, ALU.mult).then_inc(v_xn1, 1)
            dve.wait_ge(v_pair, 3)
            dve.wait_ge(v_sum, 1)
            dve.wait_ge(c_scan, 3)
            V.tensor_tensor(sc0[:].rearrange("b (s e) -> b s e", e=2)[:, :, 0], cmp[:, 6, :], cmp[:, 5, :], ALU.add).then_inc(v_sum, 1)
            dve.wait_ge(v_sum, 2)
            V.tensor_tensor_scan(lev[:], sc0[:], sc1[:], 0.0, ALU.subtract, ALU.max).then_inc(v_lev, 1)
            V.tensor_scalar(km[:], jdx[:, 0:KV], pnum[:, 1:2], None, ALU.is_equal).then_inc(c_bm, 1)
            V.tensor_scalar(bm[:], jdx[:, 0:KV], pnum[:, 2:3], None, ALU.is_equal).then_inc(c_bm, 1)
            V.tensor_scalar(identb[:], ridx[:], float(P), None, ALU.is_equal).then_inc(c_ident, 1)
            V.tensor_scalar(rmod[:], ridx[:], L - 1, None, ALU.bitwise_and).then_inc(c_mod, 1)
            dve.wait_ge(c_mod, 4)
            V.tensor_scalar(rep[:], rmod[:], 0.0, None, ALU.is_equal).then_inc(c_rep, 1)

            dve.wait_ge(p_lev, 1)
            V.tensor_scalar(oh[:].rearrange("p g s -> p (g s)"), pswt[0][:, :], pnum[:, 0:1], None, ALU.is_equal).then_inc(v_oh, 1)
            dve.wait_ge(v_oh, 1)
            V.tensor_reduce(cnt[:], oh[:].bitcast(F32), AX_X, ALU.add).then_inc(v_cnt, 1)
            dve.wait_ge(c_bm, 2)
            dve.wait_ge(p_k, 1)
            V.scalar_tensor_tensor(ktm[:].rearrange("p (k l) -> p k l", k=KV),
                                   psmisc[1][:, 0:L].unsqueeze(1).to_broadcast([P, KV, L]), SCALE,
                                   km[:].unsqueeze(2).to_broadcast([P, KV, L]), ALU.mult, ALU.mult).then_inc(v_ktm, 1)
            dve.wait_ge(v_cnt, 1)
            V.tensor_scalar(neg[:], cnt[:], 0.5, ABSENT, ALU.is_lt, ALU.mult).then_inc(v_neg, 1)
            dve.wait_ge(v_ktm, 1)
            V.tensor_copy(khi[:], ktm[:]).then_inc(v_khi, 1)
            V.tensor_tensor(cb[:], cnt[:].unsqueeze(2).to_broadcast([P, NG, BG]),
                            bm[:].unsqueeze(1).to_broadcast([P, NG, BG]), ALU.mult).then_inc(v_cb, 1)
            dve.wait_ge(v_khi, 1)
            V.tensor_tensor(klo[:], ktm[:], khi[:].bitcast(F32), ALU.subtract).then_inc(v_klo, 1)
            dve.wait_ge(p_q, 1)
            V.tensor_copy(qs[0:64, :], psg[3][0:64, 0:P]).then_inc(v_qhi, 1)
            dve.wait_ge(v_qhi, 1)
            V.tensor_tensor(qs[64:P, :], psg[3][0:64, 0:P], qs[0:64, :].bitcast(F32), ALU.subtract).then_inc(v_qs, 1)
            dve.wait_ge(p_v, 1)
            V.tensor_tensor(vo[:, 0:KVD].rearrange("p (k d) -> p k d", k=KV),
                            psg[2][:, 0:KVD].rearrange("p (k d) -> p k d", k=KV),
                            bm[:].unsqueeze(2).to_broadcast([P, KV, HD]), ALU.mult).then_inc(v_vo, 1)
            V.tensor_copy(vo[:, KVD:VW], bm[:]).then_inc(v_vo, 1)
            dve.wait_ge(p_cnt, 1)
            V.tensor_copy(cpos[:], pswt[1][:, 0:B]).then_inc(v_cpos, 1)
            V.tensor_scalar(cabs[:], pswt[1][:, 0:B], 0.5, ABSENT, ALU.is_lt, ALU.mult).then_inc(v_cpos, 1)
            V.tensor_scalar(sel4[:].rearrange("p (n l) -> p n l", l=L), jdx[0:64, :].unsqueeze(2).to_broadcast([64, GB, L]),
                            pnum[0:64, 0:1], -1.0, ALU.is_equal, ALU.mult).then_inc(c_sel, 1)
            V.tensor_scalar(ident2[:], ridx[:], float(P), 2.0, ALU.is_equal, ALU.mult).then_inc(c_ident, 1)
            V.tensor_scalar(identr[:], ridx[:], float(P), None, ALU.is_equal).then_inc(c_ident, 1)

            def threshold(w):
                dve.wait_ge(p_gam[w], 1)
                V.tensor_scalar(gam[:, 2 * w:2 * w + 2], pswt[1][:, 500:502], 0.5 / (D * F), 0.25 * EPS,
                                ALU.mult, ALU.add).then_inc(v_part, 1)
                dve.wait_ge(v_part, w + 1)
                V.tensor_tensor(thr[:, w:w + 1], gam[:, 2 * w:2 * w + 1], gam[:, 2 * w + 1:2 * w + 2], ALU.add).then_inc(v_thr, 1)

            def ternary(w, q):
                dve.wait_ge(v_thr, w + 1)
                dve.wait_ge((a_sgn, g_sgn)[w], q // 2 + 1)
                c = slice(512 * q, 512 * q + 512)
                V.scalar_tensor_tensor(tern[:, w, c], aw[:, w, c], thr[:, w:w + 1], sg[:, w, c], ALU.is_gt, ALU.mult).then_inc(v_tern, 1)

            def maxima(g):
                dve.wait_ge(p_s, g + 1)
                V.tensor_reduce(mx[:, g, :], psg[g][:, :].rearrange("p (n l) -> p n l", l=L), AX_X, ALU.max).then_inc(v_mx, 1)

            def maxima_hi(g):
                if g == 0:
                    dve.wait_ge(c_misc, 2)
                dve.wait_ge(v_mx, g + 1)
                V.tensor_copy(mxr[:, g, 0:GB], mx[:, g, :]).then_inc(v_mhi, 1)

            def maxima_lo(g):
                dve.wait_ge(v_mhi, g + 1)
                V.tensor_tensor(mxr[:, g, 32:32 + GB], mx[:, g, :], mxr[:, g, 0:GB].bitcast(F32), ALU.subtract).then_inc(v_mlo, 1)

            def inverse_sums(g):
                dve.wait_ge(p_ctx, g + 1)
                src = psg[g][:, 0:BG * VW].rearrange("p (b v) -> p b v", b=BG)
                V.reciprocal(rec[:, g, :].rearrange("p (b k) -> p b k", b=BG), src[:, :, KVD:VW]).then_inc(v_rec, 1)

            def normalise(g):
                src = psg[g][:, 0:BG * VW].rearrange("p (b v) -> p b v", b=BG)
                dve.wait_ge(v_rec, g + 1)
                V.tensor_tensor(cn[:, g, :].rearrange("p (b k d) -> p b k d", b=BG, k=KV),
                                src[:, :, 0:KVD].rearrange("p b (k d) -> p b k d", k=KV),
                                rec[:, g, :].rearrange("p (b k) -> p b k", b=BG).unsqueeze(3).to_broadcast([P, BG, KV, HD]),
                                ALU.mult).then_inc(v_cn, 1)

            def table_bias():
                dve.wait_ge(d_bo, 16)
                dve.wait_ge(d_emb4, 16)
                V.scalar_tensor_tensor(eb[:], emb4[:], EMB_SCALE, bo_bc[:], ALU.mult, ALU.add).then_inc(v_eb, 1)

            def add_table(g):
                dve.wait_ge(p_wo, g + 1)
                if g == 0:
                    dve.wait_ge(v_eb, 1)
                V.tensor_tensor(hq[:, g, :], psg[g][:, 0:D], eb[:], ALU.add).then_inc(v_hq, 1)

            def row_stats(g):
                dve.wait_ge(v_hq, g + 1)
                V.bn_stats(st2[:, g, :], hq[:, g, :]).then_inc(v_st2, 1)

            def row_moments(g):
                dve.wait_ge(v_st2, g + 1)
                V.bn_aggr(mv2[:, g, :], st2[:, g, :]).then_inc(v_mv2, 1)

            def variance_eps(g):
                dve.wait_ge(v_mv2, g + 1)
                V.tensor_scalar(ve2[:, g:g + 1], mv2[:, g, 1:2], EPS, None, ALU.add).then_inc(v_ve2, 1)

            def norm_rows(g):
                dve.wait_ge(g_rs2, g // HALF + 1)
                V.tensor_scalar(xn2[:, g, :], hq[:, g, :], mv2[:, g, 0:1], rs2[:, g:g + 1], ALU.subtract, ALU.mult).then_inc(v_xn2, 1)

            def x_lo(g):
                dve.wait_ge(a_xhi, g + 1)
                V.tensor_tensor(xlo[:, :, g, :], psg[g][:, 0:KC * P].rearrange("p (k n) -> p k n", k=KC),
                                xhi[:, :, g, :].bitcast(F32), ALU.subtract).then_inc(v_xlo, 1)

            def hidden_lo(h, j):
                n = h * FC + j
                dve.wait_ge(a_hr, n + 1)
                if n in ROUND_ON_VECTOR:
                    V.tensor_copy(hh[:, n, :], hr[:, n % NHR, :]).then_inc(v_hh, 1)
                    dve.wait_ge(v_hh, rounded_by_dve(n))
                else:
                    dve.wait_ge(a_hh, rounded_by_act(n))
                V.tensor_tensor(hl[:, n, :], hr[:, n % NHR, :], hh[:, n, :].bitcast(F32), ALU.subtract).then_inc(v_hl, 1)

            def final_lo(g):
                if g < HALF:
                    dve.wait_ge(p_acc, g + 1)
                    dve.wait_ge(g_hb, g + 1)
                    for dst in (fhi, fin):
                        V.tensor_tensor(dst[:, g, :], psmisc[g % 2][:, 0:D], hb[:, g, :], ALU.add).then_inc(v_sumf, 1)
                    dve.wait_ge(v_sumf, 2 * (g + 1))
                    V.tensor_tensor(flo[:, g, :], fin[:, g, :], fhi[:, g, :].bitcast(F32), ALU.subtract).then_inc(v_flo, 1)
                else:
                    dve.wait_ge(a_fhi, g - HALF + 1)
                    V.tensor_tensor(flo[:, g, :], psmisc[g % 2][:, 0:D], fhi[:, g, :].bitcast(F32), ALU.subtract).then_inc(v_flo, 1)

            def result(g):
                for b in range(2, BG):
                    dve.wait_ge(p_out, g * BG + b + 1)
                    ins = V.tensor_copy(osb[:, g, b, :], out_banks(g)[b][:, 0:D])
                ins.then_inc(v_out, 1)

            maxima(0)
            maxima(1)
            maxima_hi(0)
            maxima_hi(1)
            maxima_lo(0)
            maxima_lo(1)
            maxima(2)
            maxima_hi(2)
            maxima_lo(2)
            maxima(3)
            threshold(0)
            maxima_hi(3)
            maxima_lo(3)
            ternary(0, 0)
            ternary(0, 1)
            ternary(0, 2)
            inverse_sums(0)
            normalise(0)
            inverse_sums(1)
            normalise(1)
            ternary(0, 3)
            inverse_sums(2)
            table_bias()
            normalise(2)
            add_table(0)
            row_stats(0)
            add_table(1)
            row_stats(1)
            row_moments(0)
            row_moments(1)
            variance_eps(0)
            variance_eps(1)
            threshold(1)
            inverse_sums(3)
            normalise(3)
            norm_rows(0)
            norm_rows(1)
            ternary(1, 0)
            ternary(1, 1)
            x_lo(0)
            x_lo(1)
            ternary(1, 2)
            ternary(1, 3)
            add_table(2)
            add_table(3)
            row_stats(2)
            row_stats(3)
            row_moments(2)
            row_moments(3)
            variance_eps(2)
            variance_eps(3)
            hidden_lo(0, 0)
            hidden_lo(0, 1)
            norm_rows(2)
            norm_rows(3)
            hidden_lo(0, 2)
            hidden_lo(0, 3)
            hidden_lo(0, 4)
            x_lo(2)
            x_lo(3)
            hidden_lo(0, 5)
            hidden_lo(0, 6)
            hidden_lo(0, 7)
            hidden_lo(1, 0)
            final_lo(0)
            hidden_lo(1, 1)
            hidden_lo(1, 2)
            final_lo(1)
            result(0)
            hidden_lo(1, 3)
            hidden_lo(1, 4)
            hidden_lo(1, 5)
            result(1)
            hidden_lo(1, 6)
            hidden_lo(1, 7)
            final_lo(2)
            final_lo(3)
            result(2)
            result(3)

        @block.tensor
        def _(pe):
            mm = nc.tensor.matmul
            def warm_up(n):
                for _ in range(n):
                    mm(psg[0][:, :], warm[:, 0:P], warm[:], start=True, stop=True)

            pe.wait_ge(v_warm, 1)
            warm_up(10)
            pe.wait_ge(v_xn1, 1)
            pe.wait_ge(c_ident, 1)
            for k in range(KC):
                ins = nc.tensor.transpose(psmisc[0][:, k * L:(k + 1) * L], xn1[:, k * P:(k + 1) * P], identf[0:L, 0:L])
            ins.then_inc(p_xT1, 1)
            warm_up(1)
            pe.wait_ge(v_lev, 1)
            pe.wait_ge(c_sel, 1)
            levels = lev[:].rearrange("b (s e) -> b s e", e=2)[:, :, 1]
            for g in range(NG):
                ins = mm(pswt[0][:, g * S:(g + 1) * S], selb[:, g * P:(g + 1) * P], levels, start=True, stop=True)
            ins.then_inc(p_lev, 1)
            pe.wait_ge(a_xT1, 1)
            pe.wait_ge(a_wk, 1)
            for k in range(KC):
                mm(psmisc[1][:, 0:L], wk[:, k].rearrange("p r n -> p (r n)"), xT1[:, k, 0:L], start=(k == 0), stop=False)
            pe.wait_ge(a_bkr, 1)
            pe.wait_ge(c_ones, 1)
            mm(psmisc[1][:, 0:L], bkr[:].rearrange("p r n -> p (r n)"), ones[0:1, 0:L], start=False, stop=True).then_inc(p_k, 1)
            pe.wait_ge(a_wqh, KC)
            for h in range(G):
                for k in range(KC):
                    mm(psg[3][0:64, h * L:(h + 1) * L], wqh[:, k, h], xT1[:, k, 0:L], start=(h == 0 and k == 0), stop=False,
                       skip_group_check=True)
            pe.wait_ge(a_bqr, 1)
            for h in range(G):
                ins = mm(psg[3][0:64, h * L:(h + 1) * L], bqr[:, h], ones[0:1, 0:L], start=False, stop=True, skip_group_check=True)
            ins.then_inc(p_q, 1)
            pe.wait_ge(d_wv, 16)
            for k in range(KC):
                mm(psg[2][:, 0:KVD], xT1[:, k, :], wv[:, k, :], start=(k == 0), stop=False)
            pe.wait_ge(d_bv, 16)
            mm(psg[2][:, 0:KVD], ones[0:1, :], bvr[:], start=False, stop=True).then_inc(p_v, 1)
            pe.wait_ge(v_cb, 1)
            pe.wait_ge(c_rep, 1)
            mm(pswt[1][:, 0:B], rep[:], cb[:].rearrange("p g b -> p (g b)"), start=True, stop=True).then_inc(p_cnt, 1)

            def scores(g):
                if g == 0:
                    pe.wait_ge(v_qs, 1)
                    pe.wait_ge(v_klo, 1)
                    pe.wait_ge(v_neg, 1)
                    pe.wait_ge(c_ident, 2)
                if g == 2:
                    pe.wait_ge(v_vo, 1)
                mm(psg[g][:, :], qs[:], khi[:].unsqueeze(1).to_broadcast([P, BG, P]), start=True, stop=False)
                mm(psg[g][:, :], qs[:], klo[:].unsqueeze(1).to_broadcast([P, BG, P]), start=False, stop=False)
                mm(psg[g][:, :], neg[:, g:g + 1].to_broadcast([P, P]),
                   identb[:].rearrange("p (b l) -> p b l", b=BG).unsqueeze(2).to_broadcast([P, BG, KV, L]),
                   start=False, stop=True).then_inc(p_s, 1)

            def max_t(g):
                pe.wait_ge(v_mlo, g + 1)
                if g >= 2:
                    pe.wait_ge(a_ms, g - 1)
                nc.tensor.transpose(psmisc[g % 2][0:64, 0:P], mxr[:, g, :].bitcast(F32),
                                    identf[:]).then_inc(p_mt, 1)

            def scores_t(g):
                pe.wait_ge(v_mx, g + 1)
                rhs = qs[:].unsqueeze(1).to_broadcast([P, BG, P])
                mm(psg[g][:, :], khi[:], rhs, start=True, stop=False)
                mm(psg[g][:, :], klo[:], rhs, start=False, stop=True)

            def less_max(g):
                pe.wait_ge(a_ms, g + 1)
                if g == 0:
                    pe.wait_ge(c_sel, 2)
                for b in range(BG):
                    ins = mm(psg[g][:, b * P:(b + 1) * P], sel4[:, b * P:(b + 1) * P], ms[:, g, :], start=False, stop=True,
                             skip_group_check=True)
                ins.then_inc(p_et, 1)

            def context(g):
                pe.wait_ge(g_voc, g + 1)
                pe.wait_ge(a_exp, BG * (g + 1))
                for b in range(BG):
                    ins = mm(psg[g][:, b * VW:(b + 1) * VW], et[:, g, b, :], voc[:, g * BG + b, :], start=True, stop=True)
                ins.then_inc(p_ctx, 1)

            def context_t(g):
                pe.wait_ge(v_cn, g + 1)
                for b in range(2):
                    ins = nc.tensor.transpose(psg[g][:, b * P:(b + 1) * P], cn[:, g, b * P:(b + 1) * P], identf[:])
                ins.then_inc(p_cT, 1)

            def out_proj(g):
                pe.wait_ge(a_cT, 4 * (g + 1))
                if g == 0:
                    for i in range(4):
                        pe.wait_ge(d_wo[i], 16)
                for e in range(H2):
                    ins = mm(psg[g][:, 0:D], cT[:, g, e].rearrange("p b l -> p (b l)"), wo[:, e, :], start=(e == 0), stop=(e == H2 - 1))
                ins.then_inc(p_wo, 1)

            def rows_t(g):
                pe.wait_ge(v_xn2, g + 1)
                for k in range(KC):
                    ins = nc.tensor.transpose(psg[g][:, k * P:(k + 1) * P], xn2[:, g, k * P:(k + 1) * P], identf[:])
                ins.then_inc(p_xT2, 1)

            def abs_total(w):
                pe.wait_ge(a_abs, 2 * (w + 1))
                if w == 0:
                    pe.wait_ge(v_cpos, 2)
                else:
                    pe.wait_ge(v_thr, 1)
                mm(pswt[1][:, 500:502], ones[:], asum[:, 2 * w:2 * w + 2], start=True, stop=True).then_inc(p_gam[w], 1)

            def weights_t(u):
                w, i = divmod(u, 4)
                if w == 0:
                    pe.wait_ge(v_tern, i + 1)
                    if u == 1:
                        pe.wait_ge(v_thr, 2)
                    elif u >= 2:
                        pe.wait_ge(a_wt, u - 1)
                elif i < 2:
                    pe.wait_ge(v_tern, 8)
                    pe.wait_ge(v_xlo, i + 1)
                    pe.wait_ge(c_ident, 3)
                else:
                    pe.wait_ge(a_wt, u - 1)
                for jj in range(2):
                    for k in range(KC):
                        j = 2 * i + jj
                        if w == 0:
                            src = tern[:, 0, j * D + k * P:j * D + (k + 1) * P]
                        else:
                            src = tern[:, 1, k * F:(k + 1) * F].rearrange("p (f j) -> p j f", j=FC)[:, j]
                        ins = mm((pswt, psg)[w][u % 2][:, (jj * KC + k) * P:(jj * KC + k + 1) * P], src, (identb, ident2)[w][:],
                                 start=True, stop=True)
                ins.then_inc(p_wt, 1)

            def ffn1(h, j):
                n = h * FC + j
                if n < 2:
                    pe.wait_ge(a_wt, 3 + n)
                elif n == 2:
                    pe.wait_ge(a_wt, 4)
                if j == 0:
                    pe.wait_ge(v_xlo, HALF * (h + 1))
                if n >= 2:
                    pe.wait_ge(a_hr, n - 1)
                    if n - 2 not in ROUND_ON_VECTOR:
                        pe.wait_ge(a_hh, rounded_by_act(n - 2))
                for m, part in enumerate((xhi, xlo)):
                    for k in range(KC):
                        ins = mm(pswt[n % 2][:, 0:RH], w1T[:, j, k, :], part[:, k, HALF * h:HALF * (h + 1), :].rearrange("p g n -> p (g n)"),
                                 start=(m == 0 and k == 0), stop=(m == 1 and k == KC - 1))
                ins.then_inc(p_f1, 1)

            def residual(g):
                pe.wait_ge(g_hbl, g - HALF + 1)
                if g == HALF:
                    pe.wait_ge(c_ident, 4)
                pe.wait_ge(v_sumf, 2 * (g - HALF + 1))
                mm(psmisc[g % HALF][:, 0:D], identr[:], hbh[:, g, :], start=True, stop=False)
                mm(psmisc[g % HALF][:, 0:D], identr[:], hbl[:, g, :], start=False, stop=False)

            def ffn2(j, g):
                n = g // HALF * FC + j
                r = g % HALF
                pe.wait_ge(v_hl, n + 1)
                if g < HALF and j % 2 == 0:
                    pe.wait_ge(a_wt, 5 + j // 2)
                if j == 0 and g == 0:
                    pe.wait_ge(a_ms, 4)
                for m, part in enumerate((hh, hl)):
                    ins = mm(psmisc[r][:, 0:D], part[:, n, r * P:(r + 1) * P], w2T[:, j, :],
                             start=(g < HALF and j == 0 and m == 0), stop=(j == FC - 1 and m == 1))
                if j == FC - 1:
                    ins.then_inc(p_acc, 1)

            def spread(g, b):
                if b == 0:
                    pe.wait_ge(v_flo, g + 1)
                if g == 0 and b == 0:
                    pe.wait_ge(a_wt, 8)
                    pe.wait_ge(v_xlo, NG)
                if g == NG - 1 and b == 0:
                    pe.wait_ge(a_hr, NH)
                    pe.wait_ge(a_hh, rounded_by_act(NH - 1))
                elif g == NG - 1 and b == 3:
                    pe.wait_ge(a_out, g)
                elif 1 <= g < NG - 1 and b % 2 == 0:
                    pe.wait_ge((a_out, v_out)[b // 2], g)
                q = slice(L * b, L * (b + 1))
                mm(out_banks(g)[b][:, 0:D], oh[q, g, :], fhi[q, g, :], start=True, stop=False)
                mm(out_banks(g)[b][:, 0:D], oh[q, g, :], flo[q, g, :], start=False, stop=True).then_inc(p_out, 1)

            scores(0)
            scores(1)
            scores(2)
            scores(3)
            max_t(0)
            abs_total(0)
            max_t(1)
            scores_t(0)
            less_max(0)
            max_t(2)
            scores_t(1)
            scores_t(2)
            less_max(1)
            less_max(2)
            max_t(3)
            context(0)
            context(1)
            scores_t(3)
            context_t(0)
            less_max(3)
            context_t(1)
            context(2)
            out_proj(0)
            out_proj(1)
            context(3)
            weights_t(0)
            abs_total(1)
            context_t(2)
            weights_t(1)
            weights_t(2)
            context_t(3)
            rows_t(0)
            rows_t(1)
            out_proj(2)
            weights_t(3)
            out_proj(3)
            ffn1(0, 0)
            ffn1(0, 1)
            weights_t(4)
            weights_t(5)
            ffn1(0, 2)
            ffn1(0, 3)
            weights_t(6)
            weights_t(7)
            ffn1(0, 4)
            ffn2(0, 0)
            ffn2(0, 1)
            ffn1(0, 5)
            ffn2(1, 1)
            rows_t(2)
            rows_t(3)
            ffn2(1, 0)
            ffn1(0, 6)
            ffn1(0, 7)
            ffn2(2, 0)
            ffn2(3, 0)
            ffn2(2, 1)
            ffn2(3, 1)
            ffn1(1, 0)
            ffn1(1, 1)
            ffn2(4, 0)
            ffn2(5, 0)
            ffn2(6, 0)
            ffn2(7, 0)
            ffn1(1, 2)
            ffn1(1, 3)
            ffn2(4, 1)
            ffn2(5, 1)
            residual(2)
            ffn2(6, 1)
            ffn2(7, 1)
            spread(0, 0)
            spread(0, 1)
            spread(0, 2)
            spread(0, 3)
            ffn2(0, 2)
            ffn1(1, 4)
            ffn1(1, 5)
            spread(1, 0)
            spread(1, 1)
            spread(1, 2)
            spread(1, 3)
            ffn1(1, 6)
            ffn1(1, 7)
            ffn2(1, 2)
            ffn2(2, 2)
            residual(3)
            ffn2(3, 2)
            ffn2(4, 2)
            ffn2(0, 3)
            ffn2(1, 3)
            ffn2(5, 2)
            ffn2(6, 2)
            ffn2(7, 2)
            ffn2(2, 3)
            ffn2(3, 3)
            ffn2(4, 3)
            ffn2(5, 3)
            ffn2(6, 3)
            ffn2(7, 3)
            spread(2, 0)
            spread(2, 1)
            spread(2, 2)
            spread(2, 3)
            spread(3, 0)
            spread(3, 1)
            spread(3, 2)
            spread(3, 3)


_INS = ["x", "L0_tok_level_emb", "L0_attn_Wq", "L0_attn_bq", "L0_attn_Wk", "L0_attn_bk", "L0_attn_Wv", "L0_attn_bv",
        "L0_attn_Wo", "L0_attn_bo", "L0_ffn_W1", "L0_ffn_b1", "L0_ffn_W2", "L0_ffn_b2"]


def kernel(**inputs):
    import numpy as _np
    import concourse.bacc as _bacc
    from concourse import mybir as _mybir
    from concourse.bass_utils import run_bass_kernel_spmd as _run

    nc = _bacc.Bacc("TRN2", target_bir_lowering=False, num_devices=1)
    arrays, args = {}, []
    for name in _INS:
        a = _np.ascontiguousarray(inputs[name])
        arrays[f"in_{name}_dram"] = a
        args.append(nc.dram_tensor(f"in_{name}_dram", a.shape, _mybir.dt.from_np(a.dtype), kind="ExternalInput").ap())
    shape = tuple(inputs["x"].shape) + (inputs["L0_tok_level_emb"].shape[1],)
    args.append(nc.dram_tensor("out_0_dram", shape, _mybir.dt.float32, kind="ExternalOutput").ap())
    level_tower(nc, *args)
    r = _run(nc, [arrays], core_ids=[0])
    return r.results[0]["out_0_dram"]
```
